# Optimizing a Trainium2 kernel written in Bass

```python
import numpy as np
import jax
import jax.numpy as jnp

def _softmax(x, axis=-1):
    return jax.nn.softmax(x, axis=axis)

def _gelu(x):
    return jax.nn.gelu(x, approximate=True)

def _silu(x):
    return jax.nn.silu(x)

def _sigmoid(x):
    return jax.nn.sigmoid(x)

def _layernorm(x, axis=-1, eps=1e-05):
    m = jnp.mean(x, axis=axis, keepdims=True)
    v = jnp.var(x, axis=axis, keepdims=True)
    return (x - m) / jnp.sqrt(v + eps)

def _scatter_add(tgt, idx, src, axis=0):
    return tgt.at[idx].add(src)

def _segment_sum(src, seg, n):
    return jax.ops.segment_sum(src, seg, n)
kernel_name = 'mk_cond_seq_d2_seqx_r2_105166'

def setup_inputs(seed: int=0):
    np.random.seed(seed)
    _w = jnp.asarray

    def _rec_inputs():
        import jax
        import jax.numpy as jnp
        _rk = jax.random.key(seed)
        x = -0.000125 + 0.9999 * jax.random.normal(jax.random.fold_in(_rk, 1), (2, 2048, 512), jnp.float32)
        _lenS = 2048 - jax.random.randint(jax.random.fold_in(_rk, 7), (2,), 0, max(1, 2048 // 4) + 1, jnp.int32)
        _lenS2 = 2048 - jax.random.randint(jax.random.fold_in(_rk, 8), (2,), 0, max(1, 2048 // 4) + 1, jnp.int32)
        itok_B_0_15 = jax.random.randint(jax.random.fold_in(_rk, 11), (2,), 0, 16, jnp.int32)
        itok_B_0_7 = jax.random.randint(jax.random.fold_in(_rk, 12), (2,), 0, 8, jnp.int32)
        return (x, itok_B_0_15, itok_B_0_7)
    x, itok_B_0_15, itok_B_0_7 = _rec_inputs()

    def _L0_cond_setup():
        import jax, jax.numpy as jnp
        import numpy as np
        B, S, D = (32, 512, 512)
        A = 128
        E = 16
        LN_EPS = 1e-05
        key = jax.random.key(seed)
        ks = jax.random.split(key, 10)
        s = lambda fan_in: 1.0 / np.sqrt(fan_in)
        return {'hidden_states': jax.random.normal(ks[0], (B, S, D), dtype=jnp.float32), 'domain_id': jax.random.randint(ks[1], (B,), 0, E, dtype=jnp.int64), 'down_W': jax.random.uniform(ks[2], (A, D), jnp.float32, -s(D), s(D)), 'down_b': jax.random.uniform(ks[3], (A,), jnp.float32, -s(D), s(D)), 'up_W': jax.random.uniform(ks[4], (D, A), jnp.float32, -s(A), s(A)), 'up_b': jax.random.uniform(ks[5], (D,), jnp.float32, -s(A), s(A)), 'expert_W': jax.random.uniform(ks[6], (E, A, A), jnp.float32, -s(A), s(A)), 'expert_b': jax.random.uniform(ks[7], (E, A), jnp.float32, -s(A), s(A)), 'domain_emb': jax.random.normal(ks[8], (E, A), dtype=jnp.float32), 'ln_gamma': jnp.ones((D,), jnp.float32), 'ln_beta': jnp.zeros((D,), jnp.float32)}
    _L0_cond_all = _L0_cond_setup()
    _L0_cond_in = {k: v for k, v in _L0_cond_all.items() if k in ('down_W', 'down_b', 'up_W', 'up_b', 'expert_W', 'expert_b', 'domain_emb', 'ln_gamma', 'ln_beta')}
    del _L0_cond_all

    def _L1_cond_setup():
        import jax, jax.numpy as jnp
        import numpy as np
        E, H, I = (8, 512, 2048)
        B, S = (4, 512)
        LN_EPS = 1e-12
        key = jax.random.key(seed)
        ks = jax.random.split(key, 8)
        x = jax.random.normal(ks[0], (B, S, H), dtype=jnp.float32)
        expert_idx = jax.random.randint(ks[1], (B,), 0, E, dtype=jnp.int64)
        Wi = jax.random.normal(ks[2], (E, H, I), dtype=jnp.float32) * 0.02
        bi = jnp.zeros((E, I), dtype=jnp.float32)
        Wo = jax.random.normal(ks[3], (E, I, H), dtype=jnp.float32) * 0.02
        bo = jnp.zeros((E, H), dtype=jnp.float32)
        gamma = jnp.ones((E, H), dtype=jnp.float32)
        beta = jnp.zeros((E, H), dtype=jnp.float32)
        return {'input_tensor': x, 'expert_idx': expert_idx, 'Wi': Wi, 'bi': bi, 'Wo': Wo, 'bo': bo, 'gamma': gamma, 'beta': beta}
    _L1_cond_all = _L1_cond_setup()
    _L1_cond_in = {k: v for k, v in _L1_cond_all.items() if k in ('Wi', 'bi', 'Wo', 'bo', 'gamma', 'beta')}
    del _L1_cond_all
    return {'x': x, 'itok_B_0_15': itok_B_0_15, 'itok_B_0_7': itok_B_0_7, 'L0_cond_down_W': _L0_cond_in['down_W'], 'L0_cond_down_b': _L0_cond_in['down_b'], 'L0_cond_up_W': _L0_cond_in['up_W'], 'L0_cond_up_b': _L0_cond_in['up_b'], 'L0_cond_expert_W': _L0_cond_in['expert_W'], 'L0_cond_expert_b': _L0_cond_in['expert_b'], 'L0_cond_domain_emb': _L0_cond_in['domain_emb'], 'L0_cond_ln_gamma': _L0_cond_in['ln_gamma'], 'L0_cond_ln_beta': _L0_cond_in['ln_beta'], 'L1_cond_Wi': _L1_cond_in['Wi'], 'L1_cond_bi': _L1_cond_in['bi'], 'L1_cond_Wo': _L1_cond_in['Wo'], 'L1_cond_bo': _L1_cond_in['bo'], 'L1_cond_gamma': _L1_cond_in['gamma'], 'L1_cond_beta': _L1_cond_in['beta']}

def reference(x, itok_B_0_15, itok_B_0_7, L0_cond_down_W, L0_cond_down_b, L0_cond_up_W, L0_cond_up_b, L0_cond_expert_W, L0_cond_expert_b, L0_cond_domain_emb, L0_cond_ln_gamma, L0_cond_ln_beta, L1_cond_Wi, L1_cond_bi, L1_cond_Wo, L1_cond_bo, L1_cond_gamma, L1_cond_beta):
    import jax
    import jax.numpy as jnp

    def _L0_cond_ref(hidden_states, domain_id, down_W, down_b, up_W, up_b, expert_W, expert_b, domain_emb, ln_gamma, ln_beta):
        import jax, jax.numpy as jnp
        import numpy as np
        B, S, D = (32, 512, 512)
        A = 128
        E = 16
        LN_EPS = 1e-05
        residual = hidden_states
        hidden = jnp.einsum('bsd,ad->bsa', hidden_states, down_W) + down_b
        hidden = jax.nn.gelu(hidden, approximate=False)
        valid = (domain_id >= 0) & (domain_id < E)
        idx = jnp.clip(domain_id, 0, E - 1)
        Wsel = expert_W[idx]
        bsel = expert_b[idx]
        expert_out = jnp.einsum('bsa,boa->bso', hidden, Wsel) + bsel[:, None, :]
        domain_output = jnp.where(valid[:, None, None], expert_out, hidden)
        hidden = domain_output + domain_emb[idx][:, None, :]
        hidden = jnp.einsum('bsa,da->bsd', hidden, up_W) + up_b
        x = hidden + residual
        mu = jnp.mean(x, axis=-1, keepdims=True)
        var = jnp.mean(jnp.square(x - mu), axis=-1, keepdims=True)
        return (x - mu) * jax.lax.rsqrt(var + LN_EPS) * ln_gamma + ln_beta

    def _L1_cond_ref(input_tensor, expert_idx, Wi, bi, Wo, bo, gamma, beta):
        import jax, jax.numpy as jnp
        import numpy as np
        E, H, I = (8, 512, 2048)
        B, S = (4, 512)
        LN_EPS = 1e-12
        Wi_b = Wi[expert_idx]
        bi_b = bi[expert_idx]
        Wo_b = Wo[expert_idx]
        bo_b = bo[expert_idx]
        g_b = gamma[expert_idx]
        be_b = beta[expert_idx]
        h = jax.nn.gelu(jnp.einsum('bsh,bhi->bsi', input_tensor, Wi_b) + bi_b[:, None, :], approximate=False)
        o = jnp.einsum('bsi,bih->bsh', h, Wo_b) + bo_b[:, None, :]
        r = o + input_tensor
        mu = jnp.mean(r, axis=-1, keepdims=True)
        var = jnp.mean(jnp.square(r - mu), axis=-1, keepdims=True)
        y = (r - mu) * jax.lax.rsqrt(var + LN_EPS)
        return y * g_b[:, None, :] + be_b[:, None, :]
    x = _L0_cond_ref(x, itok_B_0_15, L0_cond_down_W, L0_cond_down_b, L0_cond_up_W, L0_cond_up_b, L0_cond_expert_W, L0_cond_expert_b, L0_cond_domain_emb, L0_cond_ln_gamma, L0_cond_ln_beta)
    x = _L1_cond_ref(x, itok_B_0_7, L1_cond_Wi, L1_cond_bi, L1_cond_Wo, L1_cond_bo, L1_cond_gamma, L1_cond_beta)
    return x

_drawn_inputs = setup_inputs


def setup_inputs(seed=0):
    import zlib

    import numpy as np

    out = dict(_drawn_inputs(seed))
    spreads = {'L0_cond_ln_gamma': (1.0, 0.2),
     'L0_cond_ln_beta': (0.0, 0.1),
     'L1_cond_bi': (0.0, 0.1),
     'L1_cond_bo': (0.0, 0.1),
     'L1_cond_gamma': (1.0, 0.2),
     'L1_cond_beta': (0.0, 0.1)}
    factors = {'L0_cond_down_b': 8.0}
    for name, (base, spread) in spreads.items():
        noise = np.random.default_rng([zlib.crc32(name.encode()), seed]).standard_normal(out[name].shape)
        drawn = base * np.exp(spread * noise) if base else spread * noise
        out[name] = jnp.asarray(drawn.astype(out[name].dtype))
    for name, factor in factors.items():
        out[name] = (out[name] * factor).astype(out[name].dtype)
    return out
```

```python
from contextlib import ExitStack

import concourse.bass as bass
from concourse import mybir

ALU = mybir.AluOpType
ACT = mybir.ActivationFunctionType
F32 = mybir.dt.float32
F32R = mybir.dt.float32r
I32 = mybir.dt.int32

P = 128
BATCH, SEQ, D = 2, 2048, 512
A = 128
FF = 2048
E0, E1 = 16, 8
EPS0, EPS1 = 1e-5, 1e-12
TOK = 512
SUB = TOK // P
KD = D // P
CH = FF // P
TILES = BATCH * SEQ // TOK
PER_BATCH = SEQ // TOK
WI_AHEAD, WO_AHEAD = 4, 1
WI_RING, WO_RING, H_RING = 4, 2, 4


def adapter_ffn(nc, xT_d, x_d, id0_d, id1_d, downW_d, downb_d, upW_d, upb_d, expW_d, expb_d, emb_d,
                g0_d, be0_d, w_d, bi_d, bo_d, g1_d, be1_d, out_d):
    with ExitStack() as ctx:
        def sb(name, shape, dt=F32):
            return ctx.enter_context(nc.sbuf_tensor(name, shape, dt))

        def sem(name):
            return ctx.enter_context(nc.semaphore(name))

        w_raw = sb("w_raw", [P, CH, 2, D])
        wi = sb("wi", [P, WI_RING, 2, KD, P], F32R)
        wo = sb("wo", [P, WO_RING, 2, D], F32R)
        x1t = [sb(f"x1t{i}", [P, 2, KD, TOK], F32R) for i in range(2)]
        rows = sb("rows", [P, 2, SUB, D])
        h = sb("h", [P, H_RING, 2, TOK], F32R)
        xt_raw = sb("xt_raw", [P, KD, TOK])
        xt = sb("xt", [P, 2, 2, TOK], F32R)
        hid = sb("hid", [P, 2, TOK], F32R)
        down_w = sb("down_w", [P, 2, KD, A], F32R)
        up_w = sb("up_w", [P, 2, D], F32R)
        exp_w = sb("exp_w", [P, BATCH, 2, A], F32R)
        exp_now = sb("exp_now", [P, 2, A], F32R)
        bo_now = sb("bo_now", [P, D])
        hid_b_now = sb("hid_b_now", [P, 1])
        bi_now = sb("bi_now", [P, 2, CH])
        ident = sb("ident", [P, P])
        up_b = sb("up_b", [P, D])
        g0 = sb("g0", [P, D])
        be0 = sb("be0", [P, D])
        bo = sb("bo", [P, BATCH, D])
        g1 = sb("g1", [P, BATCH, D])
        be1 = sb("be1", [P, BATCH, D])
        bi = sb("bi", [P, BATCH, CH])
        down_b = sb("down_b", [P, 1])
        exp_b = sb("exp_b", [P, BATCH])
        emb = sb("emb", [P, BATCH])
        hid_b = sb("hid_b", [P, BATCH, 1])
        ids_all = sb("ids_all", [P, BATCH], I32)
        valid = sb("valid", [P, 3, BATCH])
        ids = sb("ids", [1, 4, BATCH], I32)
        idx = sb("idx", [1, 2, BATCH], I32)
        neghalf = sb("neghalf", [P, 1])
        stats = [sb(f"stats{i}", [P, SUB, 6]) for i in range(2)]
        mv = [sb(f"mv{i}", [P, SUB, 2]) for i in range(2)]
        var = [sb(f"var{i}", [P, SUB]) for i in range(2)]
        rstd = [sb(f"rstd{i}", [P, SUB]) for i in range(2)]

        ps_h = ctx.enter_context(nc.psum_tensor("ps_h", [P, 2, TOK], F32))
        acc = ctx.enter_context(nc.psum_tensor("acc", [P, SUB, D], F32))
        ps0 = ctx.enter_context(nc.psum_tensor("ps0", [P, 2, TOK], F32))

        small_landed = sem("small_landed")
        ids_landed = sem("ids_landed")
        expw_landed = sem("expw_landed")
        vec_landed = sem("vec_landed")
        downw_landed = sem("downw_landed")
        xt_first = [sem(f"xt_first{k}") for k in range(KD)]
        xt_landed = sem("xt_landed")
        rows_landed = [sem(f"rows_landed{s}") for s in range(SUB)]
        w_landed = [sem(f"w_landed{c}") for c in range(CH)]
        y_stored = [sem(f"y_stored{s}") for s in range(SUB)]
        idx_ready = sem("idx_ready")
        setup_step = sem("setup_step")
        const_ready = sem("const_ready")
        setup_ready = sem("setup_ready")
        wi_hi, wi_lo = sem("wi_hi"), sem("wi_lo")
        wo_hi, wo_lo = sem("wo_hi"), sem("wo_lo")
        mm1_done, mm2_done = sem("mm1_done"), sem("mm2_done")
        gelu_done, h_split = sem("gelu_done"), sem("h_split")
        sum_ready = [sem("sum0_ready"), sem("sum1_ready")]
        xt_hi, xt_split = sem("xt_hi"), sem("xt_split")
        down_done, expert_done = sem("down_done"), sem("expert_done")
        up_done, turned = sem("up_done"), sem("turned")
        hid_hi, hid_split = sem("hid_hi"), sem("hid_split")
        now_ready = sem("now_ready")
        stats_seen = [sem("stats0_seen"), sem("stats1_seen")]
        xb_ready = sem("xb_ready")
        ln_step = [sem("ln0_step"), sem("ln1_step")]
        rstd_ready = [sem("rstd0_ready"), sem("rstd1_ready")]
        x1_ready, y_ready = sem("x1_ready"), sem("y_ready")
        x1t_hi, x1t_split = sem("x1t_hi"), sem("x1t_split")
        res_ready = sem("res_ready")

        def wait(eng, s, value):
            if not isinstance(value, int) or value > 0:
                eng.wait_ge(s, value)

        def ahead(t, bt, bu, c):
            return (t, bt, c) if c < CH else (t + 1, bu, c - CH)

        def for_tiles(eng, tile):
            tile(0, 0, 0, 0)
            with eng.Fori(0, (TILES - 2) // 2) as i:
                tile(2 * i + 1, 1, i // 2, (i + 1) // 2)
                tile(2 * i + 2, 0, (i + 1) // 2, (i + 1) // 2)
            tile(TILES - 1, (TILES - 1) % 2, BATCH - 1, None)

        block = ctx.enter_context(nc.Block())

        @block.sync
        def _(sp):
            sp.dma_start(ids[:, 0, :], id0_d).then_inc(ids_landed, 16)
            sp.dma_start(ids[:, 1, :], id1_d).then_inc(ids_landed, 16)
            sp.dma_start(rows[:, 1, 0, :], downW_d).then_inc(downw_landed, 16)
            for k in range(KD):
                sp.dma_start(xt_raw[:, k, :], xT_d[0, :, k, :]).then_inc(xt_first[k], 16)
            sp.dma_start(rows[:, 1, 1, :], upW_d).then_inc(vec_landed, 16)
            sp.wait_ge(idx_ready, 2)
            e1 = [sp.value_load(idx[0:1, 1, b:b + 1], min_val=0, max_val=E1 - 1) for b in range(BATCH)]
            for c in range(2):
                sp.dma_start(w_raw[:, c, :, :], w_d[e1[0], c, :, :, :]).then_inc(w_landed[c], 16)
            for s in range(SUB):
                sp.dma_start(rows[:, 0, s, :], x_d[0, s, :, :]).then_inc(rows_landed[s], 16)
            for c in range(2, 4):
                sp.dma_start(w_raw[:, c, :, :], w_d[e1[0], c, :, :, :]).then_inc(w_landed[c], 16)
            sp.wait_ge(xt_split, KD)
            sp.dma_start(xt_raw[:, :, :], xT_d[1, :, :, :]).then_inc(xt_landed, 16)
            for c in range(4, CH):
                sp.dma_start(w_raw[:, c, :, :], w_d[e1[0], c, :, :, :]).then_inc(w_landed[c], 16)
            sp.wait_ge(setup_ready, 1)
            for s in range(SUB):
                sp.wait_ge(xb_ready, s + 1)
                sp.dma_start(rows[:, 1, s, :], x_d[1, s, :, :]).then_inc(rows_landed[s], 16)

            def load_xt(u):
                sp.wait_ge(xt_split, KD * u)
                sp.dma_start(xt_raw[:, :, :], xT_d[u, :, :, :]).then_inc(xt_landed, 16)

            def store_y(t, s, parity):
                sp.wait_ge(y_ready, SUB * t + s + 1)
                sp.dma_start(out_d[t, s, :, :], rows[:, parity, s, :]).then_inc(y_stored[s], 16)

            def load_rows(u, s, parity):
                sp.wait_ge(y_stored[s], 16 * (u - 1))
                sp.dma_start(rows[:, parity, s, :], x_d[u, s, :, :]).then_inc(rows_landed[s], 16)

            def turn(t, parity, xt_too):
                if xt_too:
                    load_xt(t + 2)
                store_y(t - 1, 0, 1 - parity)
                for s in range(1, SUB):
                    store_y(t - 1, s, 1 - parity)
                    load_rows(t + 1, s - 1, 1 - parity)
                load_rows(t + 1, SUB - 1, 1 - parity)

            load_xt(2)
            for t in range(1, TILES - 1):
                turn(t, t % 2, t + 2 < TILES)
                if t % PER_BATCH == PER_BATCH - 1:
                    for c in range(CH):
                        sp.wait_ge(wi_lo, CH * t + c + 1)
                        sp.wait_ge(wo_lo, CH * t + c + 1)
                        sp.dma_start(w_raw[:, c, :, :], w_d[e1[1], c, :, :, :]).then_inc(w_landed[c], 16)
            for s in range(SUB):
                store_y(TILES - 2, s, 0)
            for s in range(SUB):
                store_y(TILES - 1, s, 1)
            for s in range(SUB):
                sp.wait_ge(y_stored[s], 16 * TILES)

        @block.gpsimd
        def _(pool):
            pool.memset(ident[:, :], 0.0).then_inc(const_ready, 1)
            pool.memset(neghalf[:, :], -0.5).then_inc(const_ready, 1)
            pool.wait_ge(const_ready, 2)
            pool.affine_select(out=ident[:, :], in_=ident[:, :], compare_op=ALU.not_equal, fill=1.0, base=0,
                               pattern=[[-1, P]], channel_multiplier=1).then_inc(const_ready, 1)

            def wi_rest(t, c):
                pool.wait_ge(wi_hi, CH * t + c + 1)
                slot = wi[:, c % WI_RING, :, :, :]
                pool.tensor_tensor(slot[:, 1], w_raw[:, c, 0, :].rearrange("p (k i) -> p k i", k=KD),
                                   slot[:, 0].bitcast(F32), ALU.subtract).then_inc(wi_lo, 1)

            def wo_rest(t, c):
                pool.wait_ge(wo_hi, CH * t + c + 1)
                slot = wo[:, c % WO_RING, :, :]
                pool.tensor_tensor(slot[:, 1], w_raw[:, c, 1, :], slot[:, 0].bitcast(F32),
                                   ALU.subtract).then_inc(wo_lo, 1)

            def inverse_root(blk, t, s):
                pool.wait_ge(ln_step[blk], 4 * (SUB * t + s) + 3)
                pool.tensor_tensor(rstd[blk][:, s:s + 1], var[blk][:, s:s + 1], neghalf[:, :],
                                   ALU.pow).then_inc(rstd_ready[blk], 1)

            def add_up_bias(u, s, parity):
                pool.wait_ge(rows_landed[s], 16 * (u + 1))
                r = rows[:, parity, s, :]
                pool.tensor_tensor(r, r, up_b[:, :], ALU.add).then_inc(xb_ready, 1)

            def add_out_bias(u, s, parity):
                pool.wait_ge(turned, SUB * u + s + 1)
                pool.wait_ge(now_ready, u + 1)
                r = rows[:, parity, s, :]
                pool.tensor_tensor(r, r, bo_now[:, :], ALU.add).then_inc(res_ready, 1)

            pool.wait_ge(vec_landed, 16 * 2)
            for s in range(SUB):
                add_up_bias(0, s, 0)
            for s in range(SUB):
                inverse_root(0, 0, s)
            for c in range(WI_AHEAD):
                wi_rest(0, c)
            for c in range(WO_AHEAD):
                wo_rest(0, c)
            for s in range(SUB):
                add_out_bias(0, s, 0)

            def tile(t, parity, bt, bu):
                more = bu is not None
                for c in range(CH):
                    if more or c + WI_AHEAD < CH:
                        wi_rest(*ahead(t, bt, bu, c + WI_AHEAD)[::2])
                    if c in (1, 2, 3, 4) and not (isinstance(t, int) and t == 0):
                        inverse_root(1, t - 1, c - 1)
                    if more and c in (6, 7, 10, 11):
                        inverse_root(0, t + 1, (6, 7, 10, 11).index(c))
                    if more or c + WO_AHEAD < CH:
                        wo_rest(*ahead(t, bt, bu, c + WO_AHEAD)[::2])
                    if more and c in (3, 4, 5, 6):
                        add_up_bias(t + 1, c - 3, 1 - parity)
                    if more and c in (8, 9, 12, 13):
                        add_out_bias(t + 1, (8, 9, 12, 13).index(c), 1 - parity)

            for_tiles(pool, tile)
            for s in range(SUB):
                inverse_root(1, TILES - 1, s)

        @block.scalar
        def _(act):
            act.dma_start(down_b[:, :], downb_d).then_inc(small_landed, 16)
            act.dma_start(ids_all[:, :], id0_d.to_broadcast([P, BATCH])).then_inc(small_landed, 16)
            act.dma_start(up_b[:, :], upb_d.to_broadcast([P, D])).then_inc(vec_landed, 16)
            act.wait_ge(idx_ready, 2)
            for b in range(BATCH):
                e0 = act.value_load(idx[0:1, 0, b:b + 1], min_val=0, max_val=E0 - 1)
                act.dma_start(rows[:, 1, 2, b * A:(b + 1) * A], expW_d[e0, :, :]).then_inc(expw_landed, 16)
                act.dma_start(exp_b[:, b:b + 1], expb_d[e0, :, :]).then_inc(expw_landed, 16)
                act.dma_start(emb[:, b:b + 1], emb_d[e0, :, :]).then_inc(expw_landed, 16)
            act.dma_start(g0[:, :], g0_d.to_broadcast([P, D])).then_inc(expw_landed, 16)
            act.dma_start(be0[:, :], be0_d.to_broadcast([P, D])).then_inc(expw_landed, 16)
            for b in range(BATCH):
                e1 = act.value_load(idx[0:1, 1, b:b + 1], min_val=0, max_val=E1 - 1)
                act.dma_start(bi[:, b, :], bi_d[e1, :, :]).then_inc(small_landed, 16)
                for dst, src in ((bo, bo_d), (g1, g1_d), (be1, be1_d)):
                    act.dma_start(dst[:, b, :], src[e1, :, :].to_broadcast([P, D])).then_inc(small_landed, 16)

            def xt_round(u, k):
                if isinstance(u, int) and u == 0:
                    act.wait_ge(xt_first[k], 16)
                else:
                    act.wait_ge(xt_landed, 16 * u)
                wait(act, down_done, KD * u + k - 1)
                act.activation(xt[:, k % 2, 0, :], xt_raw[:, k, :], ACT.Copy).then_inc(xt_hi, 1)

            def hidden(u):
                act.wait_ge(down_done, KD * (u + 1))
                act.activation(hid[:, 0, :], ps0[:, 0, :], ACT.Gelu, bias=down_b[:, :])
                act.activation(ps0[:, 0, :], ps0[:, 0, :], ACT.Gelu, bias=down_b[:, :]).then_inc(hid_hi, 1)

            def expert_out(u):
                act.wait_ge(now_ready, u + 1)
                act.wait_ge(expert_done, u + 1)
                act.activation(hid[:, 0, :], ps0[:, 1, :], ACT.Identity, bias=hid_b_now[:, :])
                act.activation(ps0[:, 1, :], ps0[:, 1, :], ACT.Identity, bias=hid_b_now[:, :]).then_inc(hid_hi, 1)

            def x1t_round(u, s, parity):
                act.wait_ge(turned, SUB * u + s + 1)
                act.activation(x1t[parity][:, 0, :, s * P:(s + 1) * P],
                               ps0[:, s % 2, :].rearrange("p (k i) -> p k i", k=KD), ACT.Copy).then_inc(x1t_hi, 1)

            def wi_round(t, bt, c):
                act.wait_ge(w_landed[c], 16 * (bt + 1))
                wait(act, mm1_done, CH * t + c - WI_RING + 1)
                act.activation(wi[:, c % WI_RING, 0, :, :],
                               w_raw[:, c, 0, :].rearrange("p (k i) -> p k i", k=KD), ACT.Copy).then_inc(wi_hi, 1)

            def wo_round(t, bt, c):
                act.wait_ge(w_landed[c], 16 * (bt + 1))
                wait(act, mm2_done, SUB * (CH * t + c - WO_RING + 1))
                act.activation(wo[:, c % WO_RING, 0, :], w_raw[:, c, 1, :], ACT.Copy).then_inc(wo_hi, 1)

            def gelu(t, c, parity):
                if c == 0:
                    act.wait_ge(now_ready, t + 1)
                act.wait_ge(mm1_done, CH * t + c + 1)
                bias = bi_now[:, parity, c:c + 1]
                act.activation(h[:, c % H_RING, 0, :], ps_h[:, c % 2, :], ACT.Gelu, bias=bias)
                act.activation(ps_h[:, c % 2, :], ps_h[:, c % 2, :], ACT.Gelu, bias=bias).then_inc(gelu_done, 1)

            for k in range(KD):
                xt_round(0, k)
            act.wait_ge(small_landed, 16 * 10)
            hidden(0)
            expert_out(0)
            for c in range(WI_AHEAD):
                wi_round(0, 0, c)
            for c in range(WO_AHEAD):
                wo_round(0, 0, c)
            for s in range(SUB):
                x1t_round(0, s, 0)
            gelu(0, 0, 0)
            gelu(0, 1, 0)

            def tile(t, parity, bt, bu):
                more = bu is not None
                for c in range(CH):
                    if more and c in (0, 1):
                        xt_round(t + 1, 2 * c)
                        xt_round(t + 1, 2 * c + 1)
                    if more or c + WI_AHEAD < CH:
                        wi_round(*ahead(t, bt, bu, c + WI_AHEAD))
                    if more or c + WO_AHEAD < CH:
                        wo_round(*ahead(t, bt, bu, c + WO_AHEAD))
                    if c + 2 < CH:
                        gelu(t, c + 2, parity)
                    elif more:
                        gelu(t + 1, c + 2 - CH, 1 - parity)
                    if more and c == 1:
                        hidden(t + 1)
                    if more and c == 3:
                        expert_out(t + 1)
                    if more and c in (7, 8, 11, 12):
                        x1t_round(t + 1, (7, 8, 11, 12).index(c), 1 - parity)

            for_tiles(act, tile)

        @block.vector
        def _(dve):
            steps = [0]

            def step(ins):
                steps[0] += 1
                ins.then_inc(setup_step, 1)
                dve.wait_ge(setup_step, steps[0])

            dve.wait_ge(ids_landed, 32)
            dve.tensor_scalar(idx[:, 0, :], ids[:, 0, :], 0.0, float(E0 - 1), ALU.max, ALU.min).then_inc(idx_ready, 1)
            step(dve.tensor_scalar(ids[:, 2, :], ids[:, 1, :], 0.0, float(E1), ALU.is_lt, ALU.mult))
            step(dve.tensor_tensor(ids[:, 3, :], ids[:, 1, :], ids[:, 2, :], ALU.add))
            dve.tensor_scalar(idx[:, 1, :], ids[:, 3, :], 0.0, float(E1 - 1), ALU.max, ALU.min).then_inc(idx_ready, 1)

            def split(dst_hi, dst_lo, src):
                step(dve.tensor_copy(dst_hi, src))
                step(dve.tensor_tensor(dst_lo, src, dst_hi.bitcast(F32), ALU.subtract))

            def chunks(a, n=KD):
                return a.rearrange("p (k i) -> p k i", k=n)

            def xt_rest(u, k):
                dve.wait_ge(xt_hi, KD * u + k + 1)
                dve.tensor_tensor(xt[:, k % 2, 1, :], xt_raw[:, k, :], xt[:, k % 2, 0, :].bitcast(F32),
                                  ALU.subtract).then_inc(xt_split, 1)

            def hid_rest(u, layer):
                dve.wait_ge(hid_hi, 2 * u + layer + 1)
                dve.tensor_tensor(hid[:, 1, :], ps0[:, layer, :], hid[:, 0, :].bitcast(F32),
                                  ALU.subtract).then_inc(hid_split, 1)

            def take_sequence(u, bu, parity):
                dve.tensor_copy(exp_now[:, :, :], exp_w[:, bu, :, :])
                dve.tensor_copy(hid_b_now[:, :], hid_b[:, bu, :])
                dve.tensor_copy(bi_now[:, parity, :], bi[:, bu, :])
                dve.tensor_copy(bo_now[:, :], bo[:, bu, :]).then_inc(now_ready, 1)

            def normalize(blk, t, s, r, gamma, beta, eps, done):
                n = 4 * (SUB * t + s)
                chain = ln_step[blk]
                dve.wait_ge(sum_ready[blk], SUB * t + s + 1)
                dve.bn_stats(stats[blk][:, s, :], r).then_inc(chain, 1)
                dve.wait_ge(chain, n + 1)
                dve.sem_inc(stats_seen[blk], 1)
                dve.bn_aggr(mv[blk][:, s, :], stats[blk][:, s, :]).then_inc(chain, 1)
                dve.wait_ge(chain, n + 2)
                dve.tensor_scalar(var[blk][:, s:s + 1], mv[blk][:, s, 1:2], eps, None, ALU.add).then_inc(chain, 1)
                dve.scalar_tensor_tensor(out=r, in0=r, scalar=mv[blk][:, s, 0:1], in1=gamma,
                                         op0=ALU.subtract, op1=ALU.mult).then_inc(chain, 1)
                dve.wait_ge(chain, n + 4)
                dve.wait_ge(rstd_ready[blk], SUB * t + s + 1)
                dve.scalar_tensor_tensor(out=r, in0=r, scalar=rstd[blk][:, s:s + 1], in1=beta,
                                         op0=ALU.mult, op1=ALU.add).then_inc(done, 1)

            def adapter_rows(u, s, parity):
                r = rows[:, parity, s, :]
                dve.wait_ge(up_done, SUB * u + s + 1)
                dve.wait_ge(xb_ready, SUB * u + s + 1)
                dve.tensor_tensor(r, ps0[:, s % 2, :], r, ALU.add).then_inc(sum_ready[0], 1)
                normalize(0, u, s, r, g0[:, :], be0[:, :], EPS0, x1_ready)

            def x1t_rest(u, s, parity):
                dve.wait_ge(x1t_hi, SUB * u + s + 1)
                part = x1t[parity][:, :, :, s * P:(s + 1) * P]
                dve.tensor_tensor(part[:, 1], chunks(ps0[:, s % 2, :]), part[:, 0].bitcast(F32),
                                  ALU.subtract).then_inc(x1t_split, 1)

            def h_rest(t, c):
                dve.wait_ge(gelu_done, CH * t + c + 1)
                dve.tensor_tensor(h[:, c % H_RING, 1, :], ps_h[:, c % 2, :], h[:, c % H_RING, 0, :].bitcast(F32),
                                  ALU.subtract).then_inc(h_split, 1)

            def take_acc(t, s, parity):
                dve.wait_ge(mm2_done, SUB * (CH * t + CH - 1) + s + 1)
                dve.wait_ge(res_ready, SUB * t + s + 1)
                r = rows[:, parity, s, :]
                dve.tensor_tensor(r, acc[:, s, :], r, ALU.add).then_inc(sum_ready[1], 1)

            def out_rows(t, bt, s, parity):
                normalize(1, t, s, rows[:, parity, s, :], g1[:, bt, :], be1[:, bt, :], EPS1, y_ready)

            dve.wait_ge(downw_landed, 16)
            split(down_w[:, 0, :, :], down_w[:, 1, :, :], chunks(rows[:, 1, 0, :]))
            for k in range(2):
                xt_rest(0, k)
            dve.wait_ge(small_landed, 16 * 10)
            step(dve.tensor_scalar(valid[:, 0, :], ids_all[:, :], 0.0, None, ALU.is_ge))
            step(dve.tensor_scalar(valid[:, 1, :], ids_all[:, :], float(E0), None, ALU.is_lt))
            step(dve.tensor_tensor(valid[:, 0, :], valid[:, 0, :], valid[:, 1, :], ALU.mult))
            step(dve.tensor_scalar(valid[:, 1, :], valid[:, 0, :], -1.0, 1.0, ALU.mult, ALU.add))
            for k in range(2, KD):
                xt_rest(0, k)
            dve.wait_ge(expw_landed, 16 * (3 * BATCH + 2))
            dve.wait_ge(const_ready, 3)
            step(dve.tensor_tensor(valid[:, 2, :], exp_b[:, :], valid[:, 0, :], ALU.mult))
            step(dve.tensor_tensor(hid_b[:, :, 0], valid[:, 2, :], emb[:, :], ALU.add))
            for b in range(BATCH):
                w = rows[:, 1, 2, b * A:(b + 1) * A]
                off = rows[:, 1, 3, b * A:(b + 1) * A]
                step(dve.tensor_scalar(off, ident[:, :], valid[:, 1, b:b + 1], None, ALU.mult))
                step(dve.scalar_tensor_tensor(out=w, in0=w, scalar=valid[:, 0, b:b + 1], in1=off,
                                              op0=ALU.mult, op1=ALU.add))
                split(exp_w[:, b, 0, :], exp_w[:, b, 1, :], w)
            take_sequence(0, 0, 0)
            hid_rest(0, 0)
            dve.wait_ge(vec_landed, 16 * 2)
            split(up_w[:, 0, :], up_w[:, 1, :], rows[:, 1, 1, :])
            dve.sem_inc(setup_ready, 1)
            hid_rest(0, 1)
            for s in range(2):
                adapter_rows(0, s, 0)
            for s in range(2):
                x1t_rest(0, s, 0)
            for s in range(2, SUB):
                adapter_rows(0, s, 0)
            for s in range(2, SUB):
                x1t_rest(0, s, 0)
            h_rest(0, 0)
            h_rest(0, 1)

            def tile(t, parity, bt, bu):
                more = bu is not None
                for c in range(CH):
                    if more and c == 0:
                        dve.wait_ge(res_ready, SUB * (t + 1))
                    if more and c in (0, 1):
                        xt_rest(t + 1, 2 * c)
                        xt_rest(t + 1, 2 * c + 1)
                    if more and c == 0:
                        take_sequence(t + 1, bu, 1 - parity)
                    if more and c == 2:
                        hid_rest(t + 1, 0)
                    if more and c == 4:
                        hid_rest(t + 1, 1)
                    if c in (1, 2, 3, 4) and not (isinstance(t, int) and t == 0):
                        out_rows(t - 1, (t - 1) // PER_BATCH, c - 1, 1 - parity)
                    if more and c in (6, 7, 10, 11):
                        adapter_rows(t + 1, (6, 7, 10, 11).index(c), 1 - parity)
                    if more and c in (8, 9, 12, 13):
                        x1t_rest(t + 1, (8, 9, 12, 13).index(c), 1 - parity)
                    if more or c + 2 < CH:
                        h_rest(*ahead(t, bt, bu, c + 2)[::2])
                for s in range(SUB):
                    take_acc(t, s, parity)

            for_tiles(dve, tile)
            for s in range(SUB):
                out_rows(TILES - 1, BATCH - 1, s, 1)

        @block.tensor
        def _(pe):
            def three(out, left, right, start, stop):
                pe.matmul(out, left[0], right[0], start=start, stop=False)
                pe.matmul(out, left[0], right[1], start=False, stop=False)
                return pe.matmul(out, left[1], right[0], start=False, stop=stop)

            def up_layer(t, c, parity):
                n = CH * t + c
                pe.wait_ge(wi_lo, n + 1)
                if c == 0:
                    pe.wait_ge(x1t_split, SUB * (t + 1))
                wait(pe, h_split, n - 1)
                for k in range(KD):
                    last = three(ps_h[:, c % 2, :], [wi[:, c % WI_RING, i, k, :] for i in (0, 1)],
                                 [x1t[parity][:, i, k, :] for i in (0, 1)], k == 0, k == KD - 1)
                last.then_inc(mm1_done, 1)

            def down_layer(t, c):
                n = CH * t + c
                pe.wait_ge(wo_lo, n + 1)
                pe.wait_ge(h_split, n + 1)
                for s in range(SUB):
                    if c == 0:
                        wait(pe, sum_ready[1], SUB * (t - 1) + s + 1)
                    three(acc[:, s, :], [h[:, c % H_RING, i, s * P:(s + 1) * P] for i in (0, 1)],
                          [wo[:, c % WO_RING, i, :] for i in (0, 1)], c == 0, c == CH - 1).then_inc(mm2_done, 1)

            def adapter_down(u, k):
                pe.wait_ge(xt_split, KD * u + k + 1)
                if k == 0:
                    wait(pe, x1t_split, SUB * u - 1)
                three(ps0[:, 0, :], [down_w[:, i, k, :] for i in (0, 1)], [xt[:, k % 2, i, :] for i in (0, 1)],
                      k == 0, k == KD - 1).then_inc(down_done, 1)

            def adapter_expert(u):
                pe.wait_ge(hid_split, 2 * u + 1)
                pe.wait_ge(now_ready, u + 1)
                wait(pe, x1t_split, SUB * u)
                three(ps0[:, 1, :], [exp_now[:, i, :] for i in (0, 1)], [hid[:, i, :] for i in (0, 1)],
                      True, True).then_inc(expert_done, 1)

            def adapter_up(u, s):
                pe.wait_ge(hid_split, 2 * u + 2)
                if s >= 2:
                    pe.wait_ge(x1t_split, SUB * u + s - 1)
                three(ps0[:, s % 2, :], [hid[:, i, s * P:(s + 1) * P] for i in (0, 1)],
                      [up_w[:, i, :] for i in (0, 1)], True, True).then_inc(up_done, 1)

            def turn(u, s, parity):
                pe.wait_ge(x1_ready, SUB * u + s + 1)
                for k in range(KD):
                    last = pe.transpose(ps0[:, s % 2, k * P:(k + 1) * P],
                                        rows[:, parity, s, k * P:(k + 1) * P], ident[:, :])
                last.then_inc(turned, 1)

            pe.wait_ge(setup_step, 2 + 2)
            for k in range(KD):
                adapter_down(0, k)
            adapter_expert(0)
            pe.wait_ge(setup_ready, 1)
            for s in range(0, SUB, 2):
                adapter_up(0, s)
                adapter_up(0, s + 1)
                turn(0, s, 0)
                turn(0, s + 1, 0)
            up_layer(0, 0, 0)
            up_layer(0, 1, 0)

            def tile(t, parity, bt, bu):
                more = bu is not None
                for c in range(CH):
                    if c + 2 < CH:
                        up_layer(t, c + 2, parity)
                    elif more:
                        up_layer(t + 1, c + 2 - CH, 1 - parity)
                    if more and c in (0, 1):
                        adapter_down(t + 1, 2 * c)
                        adapter_down(t + 1, 2 * c + 1)
                    if more and c == 3:
                        adapter_expert(t + 1)
                    if more and c in (5, 6, 9, 10):
                        adapter_up(t + 1, (5, 6, 9, 10).index(c))
                    if more and c in (7, 8, 11, 12):
                        turn(t + 1, (7, 8, 11, 12).index(c), 1 - parity)
                    down_layer(t, c)

            for_tiles(pe, tile)


def kernel(x, itok_B_0_15, itok_B_0_7, L0_cond_down_W, L0_cond_down_b, L0_cond_up_W, L0_cond_up_b,
           L0_cond_expert_W, L0_cond_expert_b, L0_cond_domain_emb, L0_cond_ln_gamma, L0_cond_ln_beta,
           L1_cond_Wi, L1_cond_bi, L1_cond_Wo, L1_cond_bo, L1_cond_gamma, L1_cond_beta):
    import numpy as np
    import concourse.bacc as bacc
    from concourse.bass_utils import run_bass_kernel_spmd

    x = np.asarray(x)
    wi = np.asarray(L1_cond_Wi).reshape(E1, KD, P, CH, P).transpose(0, 3, 2, 1, 4).reshape(E1, CH, P, 1, D)
    wo = np.asarray(L1_cond_Wo).reshape(E1, CH, P, 1, D)
    arrays = {
        "xT": x.reshape(TILES, TOK, KD, P).transpose(0, 3, 2, 1),
        "x": x.reshape(TILES, SUB, P, D),
        "id0": np.asarray(itok_B_0_15).reshape(1, BATCH),
        "id1": np.asarray(itok_B_0_7).reshape(1, BATCH),
        "down_w": np.asarray(L0_cond_down_W).reshape(A, KD, P).transpose(2, 1, 0).reshape(P, KD * A),
        "down_b": np.asarray(L0_cond_down_b).reshape(A, 1),
        "up_w": np.asarray(L0_cond_up_W).T,
        "up_b": np.asarray(L0_cond_up_b).reshape(1, D),
        "exp_w": np.asarray(L0_cond_expert_W).transpose(0, 2, 1),
        "exp_b": np.asarray(L0_cond_expert_b).reshape(E0, A, 1),
        "emb": np.asarray(L0_cond_domain_emb).reshape(E0, A, 1),
        "g0": np.asarray(L0_cond_ln_gamma).reshape(1, D),
        "be0": np.asarray(L0_cond_ln_beta).reshape(1, D),
        "w": np.concatenate([wi, wo], axis=3),
        "bi": np.asarray(L1_cond_bi).reshape(E1, CH, P).transpose(0, 2, 1),
        "bo": np.asarray(L1_cond_bo).reshape(E1, 1, D),
        "g1": np.asarray(L1_cond_gamma).reshape(E1, 1, D),
        "be1": np.asarray(L1_cond_beta).reshape(E1, 1, D),
    }
    nc = bacc.Bacc("TRN2", target_bir_lowering=False, num_devices=1, dynamic_dma_scratch_size=1024)
    ins, args = {}, []
    for name, a in arrays.items():
        a = np.ascontiguousarray(a)
        ins[f"in_{name}"] = a
        args.append(nc.dram_tensor(f"in_{name}", a.shape, mybir.dt.from_np(a.dtype), kind="ExternalInput").ap())
    args.append(nc.dram_tensor("out", (TILES, SUB, P, D), F32, kind="ExternalOutput").ap())
    adapter_ffn(nc, *args)
    got = run_bass_kernel_spmd(nc, [ins], core_ids=[0]).results[0]["out"]
    return got.reshape(BATCH, SEQ, D)
```

```python
from contextlib import ExitStack

import concourse.bass as bass
from concourse import mybir

ALU = mybir.AluOpType
ACT = mybir.ActivationFunctionType
F32 = mybir.dt.float32
F32R = mybir.dt.float32r
I32 = mybir.dt.int32

P = 128
BATCH, SEQ, D = 2, 2048, 512
A = 128
FF = 2048
E0, E1 = 16, 8
EPS0, EPS1 = 1e-5, 1e-12
TOK = 512
SUB = TOK // P
KD = D // P
CH = FF // P
TILES = BATCH * SEQ // TOK
PER_BATCH = SEQ // TOK
WI_AHEAD, WO_AHEAD = 4, 2
WI_RING, WO_RING, H_RING = 4, 4, 4
WARM = (10, 8, 8, 16, 10, 6)
LATE = 3


def adapter_ffn(nc, xT_d, x_d, ids_d, down_d, upW_d, exp_d, vec0_d, w_d, bi_d, vec1_d, out_d):
    with ExitStack() as ctx:
        def sb(name, shape, dt=F32):
            return ctx.enter_context(nc.sbuf_tensor(name, shape, dt))

        def sem(name):
            return ctx.enter_context(nc.semaphore(name))

        w_raw = sb("w_raw", [P, CH, 2, D])
        wi = sb("wi", [P, WI_RING, 2, KD, P], F32R)
        wo = sb("wo", [P, WO_RING, 2, D], F32R)
        x1t = [sb(f"x1t{i}", [P, 2, KD, TOK], F32R) for i in range(2)]
        rows = sb("rows", [P, 2, SUB, D])
        h = sb("h", [P, H_RING, 2, TOK], F32R)
        xt_raw = sb("xt_raw", [P, KD, TOK])
        xt = sb("xt", [P, 2, 2, TOK], F32R)
        hid = sb("hid", [P, 2, TOK], F32R)
        down_w = sb("down_w", [P, 2, KD, A], F32R)
        up_w = sb("up_w", [P, 2, D], F32R)
        exp_w = sb("exp_w", [P, BATCH, 2, A], F32R)
        exp_now = sb("exp_now", [P, 2, A], F32R)
        bo_now = sb("bo_now", [P, D])
        hid_b_now = sb("hid_b_now", [P, 1])
        bi_now = sb("bi_now", [P, 2, CH])
        down_raw = sb("down_raw", [P, D + 1])
        up_raw = sb("up_raw", [P, D])
        exp_raw = sb("exp_raw", [P, BATCH, A + 2])
        exp_off = sb("exp_off", [P, A])
        ident = sb("ident", [P, P])
        vec0 = sb("vec0", [P, 3, D])
        up_b, g0, be0 = vec0[:, 0, :], vec0[:, 1, :], vec0[:, 2, :]
        vec1 = sb("vec1", [P, BATCH, 3, D])
        bi = sb("bi", [P, BATCH, CH])
        hid_b = sb("hid_b", [P, BATCH, 1])
        ids_all = sb("ids_all", [P, BATCH], I32)
        valid = sb("valid", [P, 3, BATCH])
        ids = sb("ids", [1, 4, BATCH], I32)
        idx = sb("idx", [1, 2, BATCH], I32)
        warm = sb("warm", [P, 1])
        neghalf = sb("neghalf", [P, 1])
        negmean = sb("negmean", [P, SUB])
        stats = [sb(f"stats{i}", [P, SUB, 6]) for i in range(2)]
        mv = [sb(f"mv{i}", [P, SUB, 2]) for i in range(2)]
        var = [sb(f"var{i}", [P, SUB]) for i in range(2)]
        rstd = [sb(f"rstd{i}", [P, SUB]) for i in range(2)]

        ps_h = ctx.enter_context(nc.psum_tensor("ps_h", [P, 2, TOK], F32))
        acc = ctx.enter_context(nc.psum_tensor("acc", [P, SUB, D], F32))
        ps0 = ctx.enter_context(nc.psum_tensor("ps0", [P, 2, TOK], F32))

        def xt_part(u, k):
            return x1t[1][:, :, k, :] if isinstance(u, int) and u == 0 else xt[:, k % 2, :, :]

        ids_landed = sem("ids_landed")
        ids_all_landed = sem("ids_all_landed")
        down_landed, up_landed = sem("down_landed"), sem("up_landed")
        exp_landed = [sem(f"exp_landed{b}") for b in range(BATCH)]
        vec0_landed = sem("vec0_landed")
        ffn_landed = [sem(f"ffn_landed{b}") for b in range(BATCH)]
        xt_first = [sem(f"xt_first{k}") for k in range(KD)]
        xt_landed = sem("xt_landed")
        rows_landed = [sem(f"rows_landed{s}") for s in range(SUB)]
        w_landed = [sem(f"w_landed{c}") for c in range(CH)]
        y_stored = [sem(f"y_stored{s}") for s in range(SUB)]
        idx_ready = sem("idx_ready")
        setup_step = sem("setup_step")
        const_ready = sem("const_ready")
        down_w_ready, up_w_ready = sem("down_w_ready"), sem("up_w_ready")
        wi_hi, wi_lo = sem("wi_hi"), sem("wi_lo")
        wo_hi, wo_lo = sem("wo_hi"), sem("wo_lo")
        mm1_done, mm2_done = sem("mm1_done"), sem("mm2_done")
        gelu_done, h_split = sem("gelu_done"), sem("h_split")
        sum_ready = [sem("sum0_ready"), sem("sum1_ready")]
        xt_hi, xt_split = sem("xt_hi"), sem("xt_split")
        down_done, expert_done = sem("down_done"), sem("expert_done")
        up_done, turned = sem("up_done"), sem("turned")
        hid_hi, hid_split = sem("hid_hi"), sem("hid_split")
        exp_now_ready = sem("exp_now_ready")
        now_ready = sem("now_ready")
        xb_ready = sem("xb_ready")
        stats_ready = [sem("stats0_ready"), sem("stats1_ready")]
        stats_seen = [sem("stats0_seen"), sem("stats1_seen")]
        mv_ready = [sem("mv0_ready"), sem("mv1_ready")]
        var_ready = [sem("var0_ready"), sem("var1_ready")]
        centered = [sem("centered0"), sem("centered1")]
        negmean_ready, act_centered = sem("negmean_ready"), sem("act_centered")
        scaled, y_added = sem("scaled"), sem("y_added")
        rstd_ready = [sem("rstd0_ready"), sem("rstd1_ready")]
        x1_ready, y_ready = sem("x1_ready"), sem("y_ready")
        x1t_hi, x1t_split = sem("x1t_hi"), sem("x1t_split")
        res_ready = sem("res_ready")

        def wait(eng, s, value):
            if not isinstance(value, int) or value > 0:
                eng.wait_ge(s, value)

        def ahead(t, bt, bu, c):
            return (t, bt, c) if c < CH else (t + 1, bu, c - CH)

        def for_tiles(eng, tile):
            tile(0, 0, 0, 0)
            with eng.Fori(0, (TILES - 2) // 2) as i:
                tile(2 * i + 1, 1, i // 2, (i + 1) // 2)
                tile(2 * i + 2, 0, (i + 1) // 2, (i + 1) // 2)
            tile(TILES - 1, (TILES - 1) % 2, BATCH - 1, None)

        block = ctx.enter_context(nc.Block())

        @block.sync
        def _(sp):
            sp.dma_start(ids[:, 0:2, :], ids_d.rearrange("p (i b) -> p i b", b=BATCH)).then_inc(ids_landed, 16)
            sp.dma_start(down_raw[:, :], down_d).then_inc(down_landed, 16)
            for k in range(KD):
                sp.dma_start(xt_raw[:, k, :], xT_d[0, :, k, :]).then_inc(xt_first[k], 16)
            sp.dma_start(ids_all[:, :], ids_d[:, 0:BATCH].to_broadcast([P, BATCH])).then_inc(ids_all_landed, 16)
            sp.wait_ge(idx_ready, 2)
            e0 = [sp.value_load(idx[0:1, 0, b:b + 1], min_val=0, max_val=E0 - 1) for b in range(BATCH)]
            e1 = [sp.value_load(idx[0:1, 1, b:b + 1], min_val=0, max_val=E1 - 1) for b in range(BATCH)]

            def load_w(b, c):
                sp.dma_start(w_raw[:, c, :, :], w_d[e1[b], c, :, :, :]).then_inc(w_landed[c], 16)

            def load_ffn(b):
                sp.dma_start(bi[:, b, :], bi_d[e1[b], :, :]).then_inc(ffn_landed[b], 16)
                sp.dma_start(vec1[:, b, :, :], vec1_d[e1[b], :, :, :].to_broadcast([P, 3, D])).then_inc(ffn_landed[b], 16)

            sp.dma_start(exp_raw[:, 0, :], exp_d[e0[0], :, :]).then_inc(exp_landed[0], 16)
            sp.dma_start(up_raw[:, :], upW_d).then_inc(up_landed, 16)
            sp.dma_start(vec0[:, 0:1, :], vec0_d[:, 0:1, :].to_broadcast([P, 1, D])).then_inc(vec0_landed, 16)
            for s in range(SUB):
                sp.dma_start(rows[:, 0, s, :], x_d[0, s, :, :]).then_inc(rows_landed[s], 16)
            sp.dma_start(vec0[:, 1:3, :], vec0_d[:, 1:3, :].to_broadcast([P, 2, D])).then_inc(vec0_landed, 16)
            load_w(0, 0)
            load_w(0, 1)
            load_ffn(0)
            load_w(0, 2)
            load_w(0, 3)
            sp.wait_ge(xt_split, KD)
            sp.dma_start(xt_raw[:, :, :], xT_d[1, :, :, :]).then_inc(xt_landed, 16)
            for c in range(4, CH):
                load_w(0, c)
            for s in range(SUB):
                sp.wait_ge(xb_ready, s + 1)
                sp.dma_start(rows[:, 1, s, :], x_d[1, s, :, :]).then_inc(rows_landed[s], 16)
            sp.dma_start(exp_raw[:, 1, :], exp_d[e0[1], :, :]).then_inc(exp_landed[1], 16)
            load_ffn(1)

            def load_xt(u):
                sp.wait_ge(xt_split, KD * u)
                sp.dma_start(xt_raw[:, :, :], xT_d[u, :, :, :]).then_inc(xt_landed, 16)

            def store_y(t, s, parity):
                if t < TILES - 1:
                    sp.wait_ge(y_ready, SUB * t + s + 1)
                elif s < SUB - 1:
                    sp.wait_ge(y_added, s + 1)
                else:
                    sp.wait_ge(y_ready, SUB * t + 1)
                sp.dma_start(out_d[t, s, :, :], rows[:, parity, s, :]).then_inc(y_stored[s], 16)

            def load_rows(u, s, parity):
                sp.wait_ge(y_stored[s], 16 * (u - 1))
                sp.dma_start(rows[:, parity, s, :], x_d[u, s, :, :]).then_inc(rows_landed[s], 16)

            def turn(t, parity, xt_too):
                if xt_too:
                    load_xt(t + 2)
                store_y(t - 1, 0, 1 - parity)
                for s in range(1, SUB):
                    store_y(t - 1, s, 1 - parity)
                    load_rows(t + 1, s - 1, 1 - parity)
                load_rows(t + 1, SUB - 1, 1 - parity)

            load_xt(2)
            for t in range(1, TILES - 1):
                turn(t, t % 2, t + 2 < TILES)
                if t % PER_BATCH == PER_BATCH - 1:
                    for c in range(CH):
                        sp.wait_ge(wi_lo, CH * t + c + 1)
                        sp.wait_ge(wo_lo, CH * t + c + 1)
                        load_w(1, c)
            for s in range(SUB):
                store_y(TILES - 2, s, 0)
            for s in range(SUB):
                store_y(TILES - 1, s, 1)
            for s in range(SUB):
                sp.wait_ge(y_stored[s], 16 * TILES)

        @block.gpsimd
        def _(pool):
            pool.memset(ident[:, :], 0.0).then_inc(const_ready, 1)
            pool.memset(neghalf[:, :], -0.5).then_inc(const_ready, 1)
            pool.wait_ge(const_ready, 2)
            pool.affine_select(out=ident[:, :], in_=ident[:, :], compare_op=ALU.not_equal, fill=1.0, base=0,
                               pattern=[[-1, P]], channel_multiplier=1).then_inc(const_ready, 1)

            def wi_rest(t, c):
                pool.wait_ge(wi_hi, CH * t + c + 1)
                slot = wi[:, c % WI_RING, :, :, :]
                pool.tensor_tensor(slot[:, 1], w_raw[:, c, 0, :].rearrange("p (k i) -> p k i", k=KD),
                                   slot[:, 0].bitcast(F32), ALU.subtract).then_inc(wi_lo, 1)

            def wo_rest(t, c):
                pool.wait_ge(wo_hi, CH * t + c + 1)
                slot = wo[:, c % WO_RING, :, :]
                pool.tensor_tensor(slot[:, 1], w_raw[:, c, 1, :], slot[:, 0].bitcast(F32),
                                   ALU.subtract).then_inc(wo_lo, 1)

            def inverse_root(blk, t, s):
                pool.wait_ge(var_ready[blk], SUB * t + s + 1)
                pool.tensor_tensor(rstd[blk][:, s:s + 1], var[blk][:, s:s + 1], neghalf[:, :],
                                   ALU.pow).then_inc(rstd_ready[blk], 1)

            def add_up_bias(u, s, parity):
                pool.wait_ge(rows_landed[s], 16 * (u + 1))
                r = rows[:, parity, s, :]
                pool.tensor_tensor(r, r, up_b, ALU.add).then_inc(xb_ready, 1)

            def add_out_bias(u, s, parity):
                pool.wait_ge(turned, SUB * u + s + 1)
                pool.wait_ge(now_ready, u + 1)
                r = rows[:, parity, s, :]
                pool.tensor_tensor(r, r, bo_now[:, :], ALU.add).then_inc(res_ready, 1)

            def add_beta(s):
                pool.wait_ge(scaled, s + 1)
                r = rows[:, 1, s, :]
                pool.tensor_tensor(r, r, vec1[:, BATCH - 1, 2, :], ALU.add).then_inc(y_added, 1)

            pool.wait_ge(vec0_landed, 16)
            for s in range(SUB):
                add_up_bias(0, s, 0)
            wi_rest(0, 0)
            inverse_root(0, 0, 0)
            inverse_root(0, 0, 1)
            wi_rest(0, 1)
            wo_rest(0, 0)
            inverse_root(0, 0, 2)
            inverse_root(0, 0, 3)
            wi_rest(0, 2)
            wo_rest(0, 1)
            wi_rest(0, 3)
            for s in range(SUB):
                add_out_bias(0, s, 0)

            def tile(t, parity, bt, bu):
                more = bu is not None
                for c in range(CH):
                    if more or c + WI_AHEAD < CH:
                        wi_rest(*ahead(t, bt, bu, c + WI_AHEAD)[::2])
                    if c in (1, 2, 3, 4) and not (isinstance(t, int) and t == 0):
                        inverse_root(1, t - 1, c - 1)
                    if more and c in (6, 7, 10, 11):
                        inverse_root(0, t + 1, (6, 7, 10, 11).index(c))
                    if more or c + WO_AHEAD < CH:
                        wo_rest(*ahead(t, bt, bu, c + WO_AHEAD)[::2])
                    if more and c in (3, 4, 5, 6):
                        add_up_bias(t + 1, c - 3, 1 - parity)
                    if more and c in (8, 9, 12, 13):
                        add_out_bias(t + 1, (8, 9, 12, 13).index(c), 1 - parity)

            for_tiles(pool, tile)
            t = TILES - 1
            for s in range(SUB - 1):
                inverse_root(1, t, s)
                if s:
                    add_beta(s - 1)
            inverse_root(1, t, SUB - 1)
            add_beta(SUB - 2)

        @block.scalar
        def _(act):
            act.wait_ge(const_ready, 2)
            act.activation(warm[:, :], neghalf[:, :], ACT.Gelu)

            def xt_round(u, k):
                if isinstance(u, int) and u == 0:
                    act.wait_ge(xt_first[k], 16)
                else:
                    act.wait_ge(xt_landed, 16 * u)
                    act.wait_ge(down_done, KD * u + k - 1)
                act.activation(xt_part(u, k)[:, 0], xt_raw[:, k, :], ACT.Copy).then_inc(xt_hi, 1)

            def hidden(u):
                act.wait_ge(down_done, KD * (u + 1))
                act.activation(hid[:, 0, :], ps0[:, 0, :], ACT.Gelu, bias=down_raw[:, D:D + 1])
                act.activation(ps0[:, 0, :], ps0[:, 0, :], ACT.Gelu, bias=down_raw[:, D:D + 1]).then_inc(hid_hi, 1)

            def expert_out(u):
                act.wait_ge(exp_now_ready, u + 1)
                act.wait_ge(expert_done, u + 1)
                act.activation(hid[:, 0, :], ps0[:, 1, :], ACT.Identity, bias=hid_b_now[:, :])
                act.activation(ps0[:, 1, :], ps0[:, 1, :], ACT.Identity, bias=hid_b_now[:, :]).then_inc(hid_hi, 1)

            def x1t_round(u, s, parity):
                act.wait_ge(turned, SUB * u + s + 1)
                act.activation(x1t[parity][:, 0, :, s * P:(s + 1) * P],
                               ps0[:, s % 2, :].rearrange("p (k i) -> p k i", k=KD), ACT.Copy).then_inc(x1t_hi, 1)

            def wi_round(t, bt, c):
                act.wait_ge(w_landed[c], 16 * (bt + 1))
                wait(act, mm1_done, CH * t + c - WI_RING + 1)
                act.activation(wi[:, c % WI_RING, 0, :, :],
                               w_raw[:, c, 0, :].rearrange("p (k i) -> p k i", k=KD), ACT.Copy).then_inc(wi_hi, 1)

            def wo_round(t, bt, c):
                act.wait_ge(w_landed[c], 16 * (bt + 1))
                wait(act, mm2_done, SUB * (CH * t + c - WO_RING + 1))
                act.activation(wo[:, c % WO_RING, 0, :], w_raw[:, c, 1, :], ACT.Copy).then_inc(wo_hi, 1)

            def gelu(t, c, parity):
                if c == 0:
                    act.wait_ge(now_ready, t + 1)
                act.wait_ge(mm1_done, CH * t + c + 1)
                bias = bi_now[:, parity, c:c + 1]
                act.activation(h[:, c % H_RING, 0, :], ps_h[:, c % 2, :], ACT.Gelu, bias=bias)
                act.activation(ps_h[:, c % 2, :], ps_h[:, c % 2, :], ACT.Gelu, bias=bias).then_inc(gelu_done, 1)

            for k in range(KD):
                xt_round(0, k)
            act.wait_ge(down_landed, 16)
            hidden(0)
            expert_out(0)
            for c in range(WI_AHEAD):
                if c == WI_AHEAD - 1:
                    x1t_round(0, 0, 0)
                    x1t_round(0, 1, 0)
                wi_round(0, 0, c)
                if c < WO_AHEAD:
                    wo_round(0, 0, c)
            x1t_round(0, 2, 0)
            x1t_round(0, 3, 0)
            gelu(0, 0, 0)
            gelu(0, 1, 0)

            def tile(t, parity, bt, bu):
                more = bu is not None
                for c in range(CH):
                    if more and c in (0, 1):
                        xt_round(t + 1, 2 * c)
                        xt_round(t + 1, 2 * c + 1)
                    if more or c + WI_AHEAD < CH:
                        wi_round(*ahead(t, bt, bu, c + WI_AHEAD))
                    if more or c + WO_AHEAD < CH:
                        wo_round(*ahead(t, bt, bu, c + WO_AHEAD))
                    if c + 2 < CH:
                        gelu(t, c + 2, parity)
                    elif more:
                        gelu(t + 1, c + 2 - CH, 1 - parity)
                    if more and c == 1:
                        hidden(t + 1)
                    if more and c == 3:
                        expert_out(t + 1)
                    if more and c in (7, 8, 11, 12):
                        x1t_round(t + 1, (7, 8, 11, 12).index(c), 1 - parity)

            for_tiles(act, tile)
            for s in range(SUB - 1):
                act.wait_ge(negmean_ready, s + 1)
                r = rows[:, 1, s, :]
                act.activation(r, r, ACT.Identity, bias=negmean[:, s:s + 1]).then_inc(act_centered, 1)

        @block.vector
        def _(dve):
            steps = [0]

            def step(ins):
                steps[0] += 1
                ins.then_inc(setup_step, 1)
                dve.wait_ge(setup_step, steps[0])

            dve.wait_ge(ids_landed, 16)
            dve.tensor_scalar(idx[:, 0, :], ids[:, 0, :], 0.0, float(E0 - 1), ALU.max, ALU.min).then_inc(idx_ready, 1)
            step(dve.tensor_scalar(ids[:, 2, :], ids[:, 1, :], 0.0, float(E1), ALU.is_lt, ALU.mult))
            step(dve.tensor_tensor(ids[:, 3, :], ids[:, 1, :], ids[:, 2, :], ALU.add))
            dve.tensor_scalar(idx[:, 1, :], ids[:, 3, :], 0.0, float(E1 - 1), ALU.max, ALU.min).then_inc(idx_ready, 1)

            def split(dst_hi, dst_lo, src):
                step(dve.tensor_copy(dst_hi, src))
                step(dve.tensor_tensor(dst_lo, src, dst_hi.bitcast(F32), ALU.subtract))

            def chunks(a, n=KD):
                return a.rearrange("p (k i) -> p k i", k=n)

            def xt_rest(u, k):
                dve.wait_ge(xt_hi, KD * u + k + 1)
                part = xt_part(u, k)
                dve.tensor_tensor(part[:, 1], xt_raw[:, k, :], part[:, 0].bitcast(F32),
                                  ALU.subtract).then_inc(xt_split, 1)

            def hid_rest(u, layer):
                dve.wait_ge(hid_hi, 2 * u + layer + 1)
                dve.tensor_tensor(hid[:, 1, :], ps0[:, layer, :], hid[:, 0, :].bitcast(F32),
                                  ALU.subtract).then_inc(hid_split, 1)

            def take_sequence(u, bu, parity):
                dve.tensor_copy(exp_now[:, :, :], exp_w[:, bu, :, :])
                dve.tensor_copy(hid_b_now[:, :], hid_b[:, bu, :]).then_inc(exp_now_ready, 1)
                dve.tensor_copy(bi_now[:, parity, :], bi[:, bu, :])
                dve.tensor_copy(bo_now[:, :], vec1[:, bu, 0, :]).then_inc(now_ready, 1)

            def normalize(blk, t, subs, row, gamma, beta, eps, done):
                for s in subs:
                    dve.wait_ge(sum_ready[blk], SUB * t + s + 1)
                    dve.bn_stats(stats[blk][:, s, :], row(s)).then_inc(stats_ready[blk], 1)
                for s in subs:
                    dve.wait_ge(stats_ready[blk], SUB * t + s + 1)
                    dve.sem_inc(stats_seen[blk], 1)
                    dve.bn_aggr(mv[blk][:, s, :], stats[blk][:, s, :]).then_inc(mv_ready[blk], 1)
                for s in subs:
                    dve.wait_ge(mv_ready[blk], SUB * t + s + 1)
                    dve.tensor_scalar(var[blk][:, s:s + 1], mv[blk][:, s, 1:2], eps, None,
                                      ALU.add).then_inc(var_ready[blk], 1)
                for s in subs:
                    dve.scalar_tensor_tensor(out=row(s), in0=row(s), scalar=mv[blk][:, s, 0:1], in1=gamma,
                                             op0=ALU.subtract, op1=ALU.mult).then_inc(centered[blk], 1)
                for s in subs:
                    before = SUB - 1 if isinstance(t, int) and blk == 1 and t == TILES - 1 else 0
                    dve.wait_ge(centered[blk], SUB * t + s + 1 - before)
                    dve.wait_ge(rstd_ready[blk], SUB * t + s + 1)
                    dve.scalar_tensor_tensor(out=row(s), in0=row(s), scalar=rstd[blk][:, s:s + 1], in1=beta,
                                             op0=ALU.mult, op1=ALU.add).then_inc(done, 1)

            def adapter_rows(u, subs, parity, bank):
                for s in subs:
                    r = rows[:, parity, s, :]
                    dve.wait_ge(up_done, SUB * u + s + 1)
                    dve.wait_ge(xb_ready, SUB * u + s + 1)
                    dve.tensor_tensor(r, bank(s), r, ALU.add).then_inc(sum_ready[0], 1)
                normalize(0, u, subs, lambda s: rows[:, parity, s, :], g0, be0, EPS0, x1_ready)

            def x1t_rest(u, s, parity):
                dve.wait_ge(x1t_hi, SUB * u + s + 1)
                part = x1t[parity][:, :, :, s * P:(s + 1) * P]
                dve.tensor_tensor(part[:, 1], chunks(ps0[:, s % 2, :]), part[:, 0].bitcast(F32),
                                  ALU.subtract).then_inc(x1t_split, 1)

            def h_rest(t, c):
                dve.wait_ge(gelu_done, CH * t + c + 1)
                dve.tensor_tensor(h[:, c % H_RING, 1, :], ps_h[:, c % 2, :], h[:, c % H_RING, 0, :].bitcast(F32),
                                  ALU.subtract).then_inc(h_split, 1)

            def take_acc(t, s, parity):
                if isinstance(t, int) and t == TILES - 1:
                    dve.wait_ge(mm2_done, SUB * (CH * t + CH - LATE) + (s // 2) * 2 * LATE + 2 * LATE - 1 + s % 2)
                else:
                    dve.wait_ge(mm2_done, SUB * (CH * t + CH - 1) + s + 1)
                dve.wait_ge(res_ready, SUB * t + s + 1)
                r = rows[:, parity, s, :]
                dve.tensor_tensor(r, acc[:, s, :], r, ALU.add).then_inc(sum_ready[1], 1)

            def out_rows(t, bt, subs, parity):
                normalize(1, t, subs, lambda s: rows[:, parity, s, :], vec1[:, bt, 1, :], vec1[:, bt, 2, :],
                          EPS1, y_ready)

            def start_shared(t, s, parity):
                dve.wait_ge(sum_ready[1], SUB * t + s + 1)
                dve.bn_stats(stats[1][:, s, :], rows[:, parity, s, :]).then_inc(stats_ready[1], 1)
                dve.wait_ge(stats_ready[1], SUB * t + s + 1)
                dve.bn_aggr(mv[1][:, s, :], stats[1][:, s, :]).then_inc(mv_ready[1], 1)
                dve.wait_ge(mv_ready[1], SUB * t + s + 1)
                dve.tensor_scalar(negmean[:, s:s + 1], mv[1][:, s, 0:1], -1.0, None, ALU.mult).then_inc(negmean_ready, 1)
                dve.tensor_scalar(var[1][:, s:s + 1], mv[1][:, s, 1:2], EPS1, None, ALU.add).then_inc(var_ready[1], 1)

            def end_shared(t, s, parity):
                dve.wait_ge(act_centered, s + 1)
                dve.wait_ge(rstd_ready[1], SUB * t + s + 1)
                r = rows[:, parity, s, :]
                dve.scalar_tensor_tensor(out=r, in0=r, scalar=rstd[1][:, s:s + 1], in1=vec1[:, BATCH - 1, 1, :],
                                         op0=ALU.mult, op1=ALU.mult).then_inc(scaled, 1)

            def expert_matrix(b):
                dve.wait_ge(exp_landed[b], 16)
                w = exp_raw[:, b, 0:A]
                step(dve.tensor_tensor(valid[:, 2, b:b + 1], exp_raw[:, b, A:A + 1], valid[:, 0, b:b + 1], ALU.mult))
                step(dve.tensor_tensor(hid_b[:, b, :], valid[:, 2, b:b + 1], exp_raw[:, b, A + 1:A + 2], ALU.add))
                step(dve.tensor_scalar(exp_off[:, :], ident[:, :], valid[:, 1, b:b + 1], None, ALU.mult))
                step(dve.scalar_tensor_tensor(out=w, in0=w, scalar=valid[:, 0, b:b + 1], in1=exp_off[:, :],
                                              op0=ALU.mult, op1=ALU.add))
                split(exp_w[:, b, 0, :], exp_w[:, b, 1, :], w)

            dve.wait_ge(down_landed, 16)
            split(down_w[:, 0, :, :], down_w[:, 1, :, :], chunks(down_raw[:, 0:D]))
            dve.sem_inc(down_w_ready, 1)
            for k in range(KD):
                xt_rest(0, k)
            dve.wait_ge(ids_all_landed, 16)
            dve.wait_ge(const_ready, 3)
            step(dve.tensor_scalar(valid[:, 0, :], ids_all[:, :], 0.0, None, ALU.is_ge))
            step(dve.tensor_scalar(valid[:, 1, :], ids_all[:, :], float(E0), None, ALU.is_lt))
            step(dve.tensor_tensor(valid[:, 0, :], valid[:, 0, :], valid[:, 1, :], ALU.mult))
            step(dve.tensor_scalar(valid[:, 1, :], valid[:, 0, :], -1.0, 1.0, ALU.mult, ALU.add))
            expert_matrix(0)
            dve.tensor_copy(exp_now[:, :, :], exp_w[:, 0, :, :])
            dve.tensor_copy(hid_b_now[:, :], hid_b[:, 0, :]).then_inc(exp_now_ready, 1)
            hid_rest(0, 0)
            dve.wait_ge(up_landed, 16)
            split(up_w[:, 0, :], up_w[:, 1, :], up_raw[:, :])
            dve.sem_inc(up_w_ready, 1)
            hid_rest(0, 1)
            dve.wait_ge(vec0_landed, 32)
            for pair in ((0, 1), (2, 3)):
                adapter_rows(0, pair, 0, lambda s: acc[:, s, :])
                for s in pair:
                    x1t_rest(0, s, 0)
            dve.wait_ge(ffn_landed[0], 32)
            dve.tensor_copy(bi_now[:, 0, :], bi[:, 0, :])
            dve.tensor_copy(bo_now[:, :], vec1[:, 0, 0, :]).then_inc(now_ready, 1)
            h_rest(0, 0)
            h_rest(0, 1)

            def tile(t, parity, bt, bu):
                more = bu is not None
                for c in range(CH):
                    if more and c == 0:
                        dve.wait_ge(res_ready, SUB * (t + 1))
                    if more and c in (0, 1):
                        xt_rest(t + 1, 2 * c)
                        xt_rest(t + 1, 2 * c + 1)
                    if more and c == 0:
                        take_sequence(t + 1, bu, 1 - parity)
                    if more and c == 2:
                        hid_rest(t + 1, 0)
                    if more and c == 4:
                        hid_rest(t + 1, 1)
                    if c in (1, 2, 3, 4) and not (isinstance(t, int) and t == 0):
                        out_rows(t - 1, (t - 1) // PER_BATCH, (c - 1,), 1 - parity)
                    if c == 9 and isinstance(t, int) and t == 0:
                        expert_matrix(1)
                        dve.wait_ge(ffn_landed[1], 32)
                    if more and c in (6, 7, 10, 11):
                        adapter_rows(t + 1, ((6, 7, 10, 11).index(c),), 1 - parity,
                                     lambda s: ps0[:, s % 2, :])
                    if more and c in (8, 9, 12, 13):
                        x1t_rest(t + 1, (8, 9, 12, 13).index(c), 1 - parity)
                    if more or c + 2 < CH:
                        h_rest(*ahead(t, bt, bu, c + 2)[::2])
                for s in range(SUB):
                    take_acc(t, s, parity)
                    if not more and s < SUB - 1:
                        start_shared(t, s, parity)
                        if s:
                            end_shared(t, s - 1, parity)
                    elif not more:
                        end_shared(t, s - 1, parity)
                        out_rows(t, BATCH - 1, (s,), parity)

            for_tiles(dve, tile)

        @block.tensor
        def _(pe):
            def three(out, left, right, start, stop):
                pe.matmul(out, left[0], right[0], start=start, stop=False)
                pe.matmul(out, left[0], right[1], start=False, stop=False)
                return pe.matmul(out, left[1], right[0], start=False, stop=stop)

            def up_products(c, parity, a, b):
                for k in range(KD):
                    last = three(ps_h[:, c % 2, a:b], [wi[:, c % WI_RING, i, k, :] for i in (0, 1)],
                                 [x1t[parity][:, i, k, a:b] for i in (0, 1)], k == 0, k == KD - 1)
                return last

            def up_layer(t, c, parity):
                n = CH * t + c
                pe.wait_ge(wi_lo, n + 1)
                if c == 0:
                    pe.wait_ge(x1t_split, SUB * (t + 1))
                wait(pe, h_split, n - 1)
                up_products(c, parity, 0, TOK).then_inc(mm1_done, 1)

            def down_product(c, s):
                three(acc[:, s, :], [h[:, c % H_RING, i, s * P:(s + 1) * P] for i in (0, 1)],
                      [wo[:, c % WO_RING, i, :] for i in (0, 1)], c == 0, c == CH - 1).then_inc(mm2_done, 1)

            def down_layer(t, c):
                n = CH * t + c
                pe.wait_ge(wo_lo, n + 1)
                pe.wait_ge(h_split, n + 1)
                for s in range(SUB):
                    if c == 0:
                        wait(pe, sum_ready[1], SUB * (t - 1) + s + 1)
                    down_product(c, s)

            def adapter_down(u, k):
                pe.wait_ge(xt_split, KD * u + k + 1)
                if k == 0:
                    wait(pe, x1t_split, SUB * u - 1)
                three(ps0[:, 0, :], [down_w[:, i, k, :] for i in (0, 1)], [xt_part(u, k)[:, i] for i in (0, 1)],
                      k == 0, k == KD - 1).then_inc(down_done, 1)

            def adapter_expert(u):
                pe.wait_ge(hid_split, 2 * u + 1)
                pe.wait_ge(exp_now_ready, u + 1)
                wait(pe, x1t_split, SUB * u)
                three(ps0[:, 1, :], [exp_now[:, i, :] for i in (0, 1)], [hid[:, i, :] for i in (0, 1)],
                      True, True).then_inc(expert_done, 1)

            def adapter_up(u, s, bank):
                pe.wait_ge(hid_split, 2 * u + 2)
                three(bank, [hid[:, i, s * P:(s + 1) * P] for i in (0, 1)],
                      [up_w[:, i, :] for i in (0, 1)], True, True).then_inc(up_done, 1)

            def turn(u, s, parity):
                pe.wait_ge(x1_ready, SUB * u + s + 1)
                for k in range(KD):
                    last = pe.transpose(ps0[:, s % 2, k * P:(k + 1) * P],
                                        rows[:, parity, s, k * P:(k + 1) * P], ident[:, :])
                last.then_inc(turned, 1)

            def keep_warm(n, bank):
                for _ in range(n):
                    pe.matmul(bank[:, 0:P], ident[:, :], ident[:, :], start=True, stop=True)

            pe.wait_ge(const_ready, 3)
            keep_warm(WARM[0], ps_h[:, 1, :])
            pe.wait_ge(down_w_ready, 1)
            for k in range(KD):
                adapter_down(0, k)
            keep_warm(WARM[1], ps_h[:, 1, :])
            adapter_expert(0)
            keep_warm(WARM[2], ps_h[:, 1, :])
            pe.wait_ge(up_w_ready, 1)
            for s in range(SUB):
                adapter_up(0, s, acc[:, s, :])
            keep_warm(WARM[3], ps_h[:, 1, :])
            for s in range(SUB):
                if s >= 2:
                    pe.wait_ge(x1t_split, s - 1)
                turn(0, s, 0)
                if s % 2:
                    if s == SUB - 1:
                        keep_warm(WARM[5], acc[:, 0, :])
                    pe.wait_ge(x1t_split, s + 1)
                    for c in range(2):
                        pe.wait_ge(wi_lo, c + 1)
                        last = up_products(c, 0, (s - 1) * P, (s + 1) * P)
                        if s == SUB - 1:
                            last.then_inc(mm1_done, 1)
                    if s == 1:
                        keep_warm(WARM[4], acc[:, 0, :])

            def tile(t, parity, bt, bu):
                more = bu is not None
                for c in range(CH):
                    if c + 2 < CH:
                        up_layer(t, c + 2, parity)
                    elif more:
                        up_layer(t + 1, c + 2 - CH, 1 - parity)
                    if more and c in (0, 1):
                        adapter_down(t + 1, 2 * c)
                        adapter_down(t + 1, 2 * c + 1)
                    if more and c == 3:
                        adapter_expert(t + 1)
                    if more and c in (5, 6, 9, 10):
                        s = (5, 6, 9, 10).index(c)
                        if s >= 2:
                            pe.wait_ge(x1t_split, SUB * (t + 1) + s - 1)
                        adapter_up(t + 1, s, ps0[:, s % 2, :])
                    if more and c in (7, 8, 11, 12):
                        turn(t + 1, (7, 8, 11, 12).index(c), 1 - parity)
                    if more or c < CH - LATE:
                        down_layer(t, c)
                    elif c == CH - 1:
                        pe.wait_ge(wo_lo, CH * t + c)
                        pe.wait_ge(h_split, CH * t + c)
                        for pair in ((0, 1), (2, 3)):
                            for s in pair:
                                for j in range(CH - LATE, c):
                                    down_product(j, s)
                            if pair[0] == 0:
                                pe.wait_ge(wo_lo, CH * t + c + 1)
                                pe.wait_ge(h_split, CH * t + c + 1)
                            for s in pair:
                                down_product(c, s)

            for_tiles(pe, tile)


def kernel(x, itok_B_0_15, itok_B_0_7, L0_cond_down_W, L0_cond_down_b, L0_cond_up_W, L0_cond_up_b,
           L0_cond_expert_W, L0_cond_expert_b, L0_cond_domain_emb, L0_cond_ln_gamma, L0_cond_ln_beta,
           L1_cond_Wi, L1_cond_bi, L1_cond_Wo, L1_cond_bo, L1_cond_gamma, L1_cond_beta):
    import numpy as np
    import concourse.bacc as bacc
    from concourse.bass_utils import run_bass_kernel_spmd

    x = np.asarray(x)
    wi = np.asarray(L1_cond_Wi).reshape(E1, KD, P, CH, P).transpose(0, 3, 2, 1, 4).reshape(E1, CH, P, 1, D)
    wo = np.asarray(L1_cond_Wo).reshape(E1, CH, P, 1, D)
    arrays = {
        "xT": x.reshape(TILES, TOK, KD, P).transpose(0, 3, 2, 1),
        "x": x.reshape(TILES, SUB, P, D),
        "ids": np.concatenate([np.asarray(itok_B_0_15), np.asarray(itok_B_0_7)]).reshape(1, 2 * BATCH),
        "down": np.concatenate([np.asarray(L0_cond_down_W).reshape(A, KD, P).transpose(2, 1, 0).reshape(P, KD * A),
                                np.asarray(L0_cond_down_b).reshape(A, 1)], axis=1),
        "up_w": np.asarray(L0_cond_up_W).T,
        "exp": np.concatenate([np.asarray(L0_cond_expert_W).transpose(0, 2, 1),
                               np.asarray(L0_cond_expert_b).reshape(E0, A, 1),
                               np.asarray(L0_cond_domain_emb).reshape(E0, A, 1)], axis=2),
        "vec0": np.stack([np.asarray(L0_cond_up_b), np.asarray(L0_cond_ln_gamma),
                          np.asarray(L0_cond_ln_beta)]).reshape(1, 3, D),
        "w": np.concatenate([wi, wo], axis=3),
        "bi": np.asarray(L1_cond_bi).reshape(E1, CH, P).transpose(0, 2, 1),
        "vec1": np.stack([np.asarray(L1_cond_bo), np.asarray(L1_cond_gamma),
                          np.asarray(L1_cond_beta)], axis=1).reshape(E1, 1, 3, D),
    }
    nc = bacc.Bacc("TRN2", target_bir_lowering=False, num_devices=1, dynamic_dma_scratch_size=1024)
    ins, args = {}, []
    for name, a in arrays.items():
        a = np.ascontiguousarray(a)
        ins[f"in_{name}"] = a
        args.append(nc.dram_tensor(f"in_{name}", a.shape, mybir.dt.from_np(a.dtype), kind="ExternalInput").ap())
    args.append(nc.dram_tensor("out", (TILES, SUB, P, D), F32, kind="ExternalOutput").ap())
    adapter_ffn(nc, *args)
    got = run_bass_kernel_spmd(nc, [ins], core_ids=[0]).results[0]["out"]
    return got.reshape(BATCH, SEQ, D)
```

```python
from contextlib import ExitStack

import concourse.bass as bass
from concourse import mybir

ALU = mybir.AluOpType
ACT = mybir.ActivationFunctionType
F32 = mybir.dt.float32
F32R = mybir.dt.float32r
I32 = mybir.dt.int32

P = 128
BATCH, SEQ, D = 2, 2048, 512
A = 128
FF = 2048
E0, E1 = 16, 8
EPS0, EPS1 = 1e-5, 1e-12
TOK = 512
SUB = TOK // P
KD = D // P
CH = FF // P
BLK = 32
TILES = BATCH * SEQ // TOK
PER_BATCH = SEQ // TOK
WI_AHEAD, WO_AHEAD = 4, 2
WI_RING, WO_RING, H_RING = 4, 4, 4
UP_AT, NORM_AT, TURN_AT, SPLIT_AT = (4, 6, 8, 10), (5, 7, 9, 11), (6, 8, 10, 12), (7, 9, 11, 13)
WARM = (11, 1, 7, 8)
EARLY = 4
LATE = 4


def adapter_ffn(nc, xT_d, x_d, ids_d, down_d, upW_d, exp_d, vec0_d, w_d, bi_d, vec1_d, out_d):
    with ExitStack() as ctx:
        def sb(name, shape, dt=F32):
            return ctx.enter_context(nc.sbuf_tensor(name, shape, dt))

        def sem(name):
            return ctx.enter_context(nc.semaphore(name))

        w_raw = sb("w_raw", [P, CH, 2, D])
        wi = sb("wi", [P, WI_RING, 2, KD, P], F32R)
        wo = sb("wo", [P, WO_RING, 2, D], F32R)
        x1t = [sb(f"x1t{i}", [P, 2, KD, TOK], F32R) for i in range(2)]
        rows = sb("rows", [P, 2, SUB, D])
        h = sb("h", [P, H_RING, 2, TOK], F32R)
        xt_raw = sb("xt_raw", [P, KD, TOK])
        xt = sb("xt", [P, 2, 2, TOK], F32R)
        hid = sb("hid", [P, 2, TOK], F32R)
        down_w = sb("down_w", [P, 2, KD, A], F32R)
        up_w = sb("up_w", [P, 2, D], F32R)
        exp_w = sb("exp_w", [P, 2, A], F32R)
        exp_b = sb("exp_b", [P, 2, P], F32R)
        fold_w = sb("fold_w", [P, BATCH, 2, D], F32R)
        bi_now = sb("bi_now", [P, 2, CH])
        down_raw = sb("down_raw", [P, D + 1])
        up_raw = rows[:, 1, 0, :]
        exp_raw = sb("exp_raw", [P, BATCH, A + 2])
        exp_off = down_raw[:, 0:A]
        ident = sb("ident", [P, P])
        up_b = sb("up_b", [P, BATCH, D])
        vec0 = sb("vec0", [P, 2, D])
        g0, be0 = vec0[:, 0, :], vec0[:, 1, :]
        vec1 = sb("vec1", [P, BATCH, 3, D])
        bi = sb("bi", [P, BATCH, CH])
        hid_b = sb("hid_b", [P, 1])
        ids_all = sb("ids_all", [P, BATCH], I32)
        valid = sb("valid", [P, 3, BATCH])
        ids = sb("ids", [1, 4, BATCH], I32)
        idx = sb("idx", [1, 2, BATCH], I32)
        warm = sb("warm", [P, 1])
        neghalf = sb("neghalf", [P, 1])
        negmean = sb("negmean", [P, SUB])
        stats = [sb(f"stats{i}", [P, SUB, 6]) for i in range(2)]
        mv = [sb(f"mv{i}", [P, SUB, 2]) for i in range(2)]
        var = [sb(f"var{i}", [P, SUB]) for i in range(2)]
        rstd = [sb(f"rstd{i}", [P, SUB]) for i in range(2)]

        ps_h = ctx.enter_context(nc.psum_tensor("ps_h", [P, 2, TOK], F32))
        acc = ctx.enter_context(nc.psum_tensor("acc", [P, SUB, D], F32))
        ps0 = ctx.enter_context(nc.psum_tensor("ps0", [P, 2, TOK], F32))

        def xt_part(u, k):
            return x1t[1][:, :, k, :] if isinstance(u, int) and u == 0 else xt[:, k % 2, :, :]

        def hidden_bank(t, c):
            return acc[:, c - 2, :] if isinstance(t, int) and t == 0 and c in (2, 3) else ps_h[:, c % 2, :]

        ids_landed = sem("ids_landed")
        ids_all_landed = sem("ids_all_landed")
        down_landed, up_landed, up_b_landed = sem("down_landed"), sem("up_landed"), sem("up_b_landed")
        exp_landed = [sem(f"exp_landed{b}") for b in range(BATCH)]
        vec0_landed = sem("vec0_landed")
        ffn_landed = [sem(f"ffn_landed{b}") for b in range(BATCH)]
        xt_first = [sem(f"xt_first{k}") for k in range(KD)]
        xt_landed = sem("xt_landed")
        rows_landed = [sem(f"rows_landed{s}") for s in range(SUB)]
        w_landed = [sem(f"w_landed{c}") for c in range(CH)]
        y_stored = [sem(f"y_stored{s}") for s in range(SUB)]
        idx_ready = sem("idx_ready")
        setup_step = sem("setup_step")
        const_ready = sem("const_ready")
        down_w_hi, down_w_ready = sem("down_w_hi"), sem("down_w_ready")
        up_w_hi, up_w_ready = sem("up_w_hi"), sem("up_w_ready")
        exp_w_ready, exp_b_ready = sem("exp_w_ready"), sem("exp_b_ready")
        fold_done, fold_hi, fold_split = sem("fold_done"), sem("fold_hi"), sem("fold_split")
        bias_done, up_b_ready = sem("bias_done"), sem("up_b_ready")
        wi_hi, wi_lo = sem("wi_hi"), sem("wi_lo")
        wo_hi, wo_lo = sem("wo_hi"), sem("wo_lo")
        mm1_done, mm2_done = sem("mm1_done"), sem("mm2_done")
        gelu_done, h_split = sem("gelu_done"), sem("h_split")
        sum_ready = [sem("sum0_ready"), sem("sum1_ready")]
        xt_hi, xt_split = sem("xt_hi"), sem("xt_split")
        down_done = sem("down_done")
        up_done, turned = sem("up_done"), sem("turned")
        hid_hi, hid_split = sem("hid_hi"), sem("hid_split")
        bi_now_ready = sem("bi_now_ready")
        rows_seen, turned_seen = sem("rows_seen"), sem("turned_seen")
        xb_ready = sem("xb_ready")
        stats_ready = [sem("stats0_ready"), sem("stats1_ready")]
        stats_seen = [sem("stats0_seen"), sem("stats1_seen")]
        mv_ready = [sem("mv0_ready"), sem("mv1_ready")]
        var_ready = [sem("var0_ready"), sem("var1_ready")]
        centered = [sem("centered0"), sem("centered1")]
        negmean_ready, act_centered = sem("negmean_ready"), sem("act_centered")
        act_scaled, dve_scaled = sem("act_scaled"), sem("dve_scaled")
        times_gamma_done, y_added = sem("times_gamma_done"), sem("y_added")
        rstd_ready = [sem("rstd0_ready"), sem("rstd1_ready")]
        x1_ready, y_ready = sem("x1_ready"), sem("y_ready")
        x1t_hi, x1t_split = sem("x1t_hi"), sem("x1t_split")
        res_ready = sem("res_ready")

        def wait(eng, s, value):
            if not isinstance(value, int) or value > 0:
                eng.wait_ge(s, value)

        def ahead(t, bt, bu, c):
            return (t, bt, c) if c < CH else (t + 1, bu, c - CH)

        def for_tiles(eng, tile):
            tile(0, 0, 0, 0)
            with eng.Fori(0, (TILES - 2) // 2) as i:
                tile(2 * i + 1, 1, i // 2, (i + 1) // 2)
                tile(2 * i + 2, 0, (i + 1) // 2, (i + 1) // 2)
            tile(TILES - 1, (TILES - 1) % 2, BATCH - 1, None)

        block = ctx.enter_context(nc.Block())

        @block.sync
        def _(sp):
            sp.dma_start(ids[:, 0:2, :], ids_d.rearrange("p (i b) -> p i b", b=BATCH)).then_inc(ids_landed, 16)
            sp.dma_start(down_raw[:, :], down_d).then_inc(down_landed, 16)
            for k in range(KD):
                sp.dma_start(xt_raw[:, k, :], xT_d[0, :, k, :]).then_inc(xt_first[k], 16)
                if k == 0:
                    sp.dma_start(ids_all[:, :], ids_d[:, 0:BATCH].to_broadcast([P, BATCH])).then_inc(ids_all_landed, 16)
            sp.dma_start(up_raw, upW_d).then_inc(up_landed, 16)
            sp.dma_start(up_b[:, 1:2, :], vec0_d[:, 0:1, :].to_broadcast([P, 1, D])).then_inc(up_b_landed, 16)
            sp.wait_ge(idx_ready, 2)
            e0 = [sp.value_load(idx[0:1, 0, b:b + 1], min_val=0, max_val=E0 - 1) for b in range(BATCH)]
            e1 = [sp.value_load(idx[0:1, 1, b:b + 1], min_val=0, max_val=E1 - 1) for b in range(BATCH)]

            def load_w(b, c):
                sp.dma_start(w_raw[:, c, :, :], w_d[e1[b], c, :, :, :]).then_inc(w_landed[c], 16)

            def load_ffn(b):
                sp.dma_start(bi[:, b, :], bi_d[e1[b], :, :]).then_inc(ffn_landed[b], 16)
                sp.dma_start(vec1[:, b, :, :], vec1_d[e1[b], :, :, :].to_broadcast([P, 3, D])).then_inc(ffn_landed[b], 16)

            sp.dma_start(exp_raw[:, 0, :], exp_d[e0[0], :, :]).then_inc(exp_landed[0], 16)
            for s in range(SUB):
                sp.dma_start(rows[:, 0, s, :], x_d[0, s, :, :]).then_inc(rows_landed[s], 16)
            sp.dma_start(vec0[:, :, :], vec0_d[:, 1:3, :].to_broadcast([P, 2, D])).then_inc(vec0_landed, 16)
            load_w(0, 0)
            load_w(0, 1)
            load_ffn(0)
            load_w(0, 2)
            load_w(0, 3)
            sp.dma_start(exp_raw[:, 1, :], exp_d[e0[1], :, :]).then_inc(exp_landed[1], 16)
            sp.wait_ge(xt_split, KD)
            sp.dma_start(xt_raw[:, :, :], xT_d[1, :, :, :]).then_inc(xt_landed, 16)
            for c in range(4, CH):
                load_w(0, c)
            for s in range(SUB):
                sp.wait_ge(xb_ready, s + 1)
                sp.dma_start(rows[:, 1, s, :], x_d[1, s, :, :]).then_inc(rows_landed[s], 16)
            load_ffn(1)

            def load_xt(u):
                sp.wait_ge(xt_split, KD * u)
                sp.dma_start(xt_raw[:, :, :], xT_d[u, :, :, :]).then_inc(xt_landed, 16)

            def store_y(t, s, parity):
                if t < TILES - 1:
                    sp.wait_ge(y_ready, SUB * t + s + 1)
                elif s < SUB - 1:
                    sp.wait_ge(y_added, s + 1)
                else:
                    sp.wait_ge(y_ready, SUB * t + 1)
                sp.dma_start(out_d[t, s, :, :], rows[:, parity, s, :]).then_inc(y_stored[s], 16)

            def load_rows(u, s, parity):
                sp.wait_ge(y_stored[s], 16 * (u - 1))
                sp.dma_start(rows[:, parity, s, :], x_d[u, s, :, :]).then_inc(rows_landed[s], 16)

            def turn(t, parity, xt_too):
                if xt_too:
                    load_xt(t + 2)
                store_y(t - 1, 0, 1 - parity)
                for s in range(1, SUB):
                    store_y(t - 1, s, 1 - parity)
                    load_rows(t + 1, s - 1, 1 - parity)
                load_rows(t + 1, SUB - 1, 1 - parity)

            load_xt(2)
            for t in range(1, TILES - 1):
                turn(t, t % 2, t + 2 < TILES)
                if t % PER_BATCH == PER_BATCH - 1:
                    for c in range(CH):
                        sp.wait_ge(wi_lo, CH * t + c + 1)
                        sp.wait_ge(wo_lo, CH * t + c + 1)
                        load_w(1, c)
            for s in range(SUB):
                store_y(TILES - 2, s, 0)
            for s in range(SUB):
                store_y(TILES - 1, s, 1)
            for s in range(SUB):
                sp.wait_ge(y_stored[s], 16 * TILES)

        @block.gpsimd
        def _(pool):
            pool.memset(ident[:, :], 0.0).then_inc(const_ready, 1)
            pool.memset(neghalf[:, :], -0.5).then_inc(const_ready, 1)
            pool.wait_ge(const_ready, 2)
            pool.affine_select(out=ident[:, :], in_=ident[:, :], compare_op=ALU.not_equal, fill=1.0, base=0,
                               pattern=[[-1, P]], channel_multiplier=1).then_inc(const_ready, 1)

            def wi_rest(t, c):
                pool.wait_ge(wi_hi, CH * t + c + 1)
                slot = wi[:, c % WI_RING, :, :, :]
                pool.tensor_tensor(slot[:, 1], w_raw[:, c, 0, :].rearrange("p (k i) -> p k i", k=KD),
                                   slot[:, 0].bitcast(F32), ALU.subtract).then_inc(wi_lo, 1)

            def wo_rest(t, c):
                pool.wait_ge(wo_hi, CH * t + c + 1)
                slot = wo[:, c % WO_RING, :, :]
                pool.tensor_tensor(slot[:, 1], w_raw[:, c, 1, :], slot[:, 0].bitcast(F32),
                                   ALU.subtract).then_inc(wo_lo, 1)

            def inverse_root(blk, t, s):
                pool.wait_ge(var_ready[blk], SUB * t + s + 1)
                pool.tensor_tensor(rstd[blk][:, s:s + 1], var[blk][:, s:s + 1], neghalf[:, :],
                                   ALU.pow).then_inc(rstd_ready[blk], 1)

            def add_up_bias(u, bu, s, parity):
                pool.wait_ge(rows_landed[s], 16 * (u + 1))
                pool.sem_inc(rows_seen, 1)
                r = rows[:, parity, s, :]
                pool.tensor_tensor(r, r, up_b[:, bu, :], ALU.add).then_inc(xb_ready, 1)

            def add_out_bias(u, bu, s, parity):
                pool.wait_ge(turned, SUB * u + s + 1)
                pool.sem_inc(turned_seen, 1)
                r = rows[:, parity, s, :]
                pool.tensor_tensor(r, r, vec1[:, bu, 0, :], ALU.add).then_inc(res_ready, 1)

            def times_gamma(s):
                pool.wait_ge(act_centered, s + 1)
                r = rows[:, 1, s, :]
                pool.tensor_tensor(r, r, vec1[:, BATCH - 1, 1, :], ALU.mult).then_inc(times_gamma_done, 1)

            def add_beta(s, scaled, count):
                pool.wait_ge(scaled, count)
                r = rows[:, 1, s, :]
                pool.tensor_tensor(r, r, vec1[:, BATCH - 1, 2, :], ALU.add).then_inc(y_added, 1)

            pool.wait_ge(down_w_hi, 1)
            pool.tensor_tensor(down_w[:, 1, :, :], down_raw[:, 0:D].rearrange("p (k i) -> p k i", k=KD),
                               down_w[:, 0, :, :].bitcast(F32), ALU.subtract).then_inc(down_w_ready, 1)
            pool.wait_ge(up_w_hi, 1)
            pool.tensor_tensor(up_w[:, 1, :], up_raw, up_w[:, 0, :].bitcast(F32), ALU.subtract).then_inc(up_w_ready, 1)
            pool.wait_ge(up_b_landed, 16)
            for s in range(SUB):
                add_up_bias(0, 1, s, 0)
            inverse_root(0, 0, 0)
            inverse_root(0, 0, 1)
            wi_rest(0, 0)
            wi_rest(0, 1)
            wi_rest(0, 2)
            wi_rest(0, 3)
            inverse_root(0, 0, 2)
            inverse_root(0, 0, 3)
            wo_rest(0, 0)
            wo_rest(0, 1)
            pool.wait_ge(up_b_ready, 1)
            pool.wait_ge(ffn_landed[0], 32)
            for s in range(SUB):
                add_out_bias(0, 0, s, 0)

            def tile(t, parity, bt, bu):
                more = bu is not None
                for c in range(CH):
                    if more or c + WI_AHEAD < CH:
                        wi_rest(*ahead(t, bt, bu, c + WI_AHEAD)[::2])
                    if c in (1, 2, 3, 4) and not (isinstance(t, int) and t == 0):
                        inverse_root(1, t - 1, c - 1)
                    if more and c in NORM_AT:
                        inverse_root(0, t + 1, NORM_AT.index(c))
                    if more or c + WO_AHEAD < CH:
                        wo_rest(*ahead(t, bt, bu, c + WO_AHEAD)[::2])
                    if more and c in (3, 4, 5, 6):
                        add_up_bias(t + 1, bu, c - 3, 1 - parity)
                    if more and c in SPLIT_AT:
                        add_out_bias(t + 1, bu, SPLIT_AT.index(c), 1 - parity)
                    if isinstance(t, int) and t == 0 and c == CH - 1:
                        pool.wait_ge(up_b_ready, 2)
                        pool.wait_ge(ffn_landed[1], 32)

            for_tiles(pool, tile)
            t = TILES - 1
            inverse_root(1, t, 0)
            times_gamma(0)
            inverse_root(1, t, 1)
            add_beta(0, act_scaled, 1)
            add_beta(1, dve_scaled, 1)
            inverse_root(1, t, 2)
            times_gamma(2)
            inverse_root(1, t, 3)
            add_beta(2, act_scaled, 2)

        @block.scalar
        def _(act):
            act.wait_ge(const_ready, 2)
            act.activation(warm[:, :], neghalf[:, :], ACT.Gelu)

            def xt_round(u, k):
                if isinstance(u, int) and u == 0:
                    act.wait_ge(xt_first[k], 16)
                else:
                    act.wait_ge(xt_landed, 16 * u)
                    act.wait_ge(down_done, KD * u + k - 1)
                act.activation(xt_part(u, k)[:, 0], xt_raw[:, k, :], ACT.Copy).then_inc(xt_hi, 1)

            def hidden(u):
                act.wait_ge(down_done, KD * (u + 1))
                act.activation(hid[:, 0, :], ps0[:, 0, :], ACT.Gelu, bias=down_raw[:, D:D + 1])
                act.activation(ps0[:, 0, :], ps0[:, 0, :], ACT.Gelu, bias=down_raw[:, D:D + 1]).then_inc(hid_hi, 1)

            def fold_round(b):
                act.wait_ge(fold_done, b + 1)
                act.activation(fold_w[:, b, 0, :], ps0[:, 1, :], ACT.Copy).then_inc(fold_hi, 1)

            def x1t_round(u, s, parity):
                act.wait_ge(turned, SUB * u + s + 1)
                act.activation(x1t[parity][:, 0, :, s * P:(s + 1) * P],
                               ps0[:, s % 2, :].rearrange("p (k i) -> p k i", k=KD), ACT.Copy).then_inc(x1t_hi, 1)

            def wi_round(t, bt, c):
                act.wait_ge(w_landed[c], 16 * (bt + 1))
                wait(act, mm1_done, CH * t + c - WI_RING + 1)
                act.activation(wi[:, c % WI_RING, 0, :, :],
                               w_raw[:, c, 0, :].rearrange("p (k i) -> p k i", k=KD), ACT.Copy).then_inc(wi_hi, 1)

            def wo_round(t, bt, c):
                act.wait_ge(w_landed[c], 16 * (bt + 1))
                wait(act, mm2_done, SUB * (CH * t + c - WO_RING + 1))
                act.activation(wo[:, c % WO_RING, 0, :], w_raw[:, c, 1, :], ACT.Copy).then_inc(wo_hi, 1)

            def gelu(t, c, parity):
                if c == 0:
                    act.wait_ge(bi_now_ready, t + 1)
                act.wait_ge(mm1_done, CH * t + c + 1)
                bias = bi_now[:, parity, c:c + 1]
                bank = hidden_bank(t, c)
                act.activation(h[:, c % H_RING, 0, :], bank, ACT.Gelu, bias=bias)
                act.activation(bank, bank, ACT.Gelu, bias=bias).then_inc(gelu_done, 1)

            for k in range(KD):
                xt_round(0, k)
            act.wait_ge(up_landed, 16)
            act.activation(up_w[:, 0, :], up_raw, ACT.Copy).then_inc(up_w_hi, 1)
            act.wait_ge(down_landed, 16)
            hidden(0)
            fold_round(0)
            wi_round(0, 0, 0)
            wi_round(0, 0, 1)
            x1t_round(0, 0, 0)
            x1t_round(0, 1, 0)
            for c in range(2, WI_AHEAD):
                wi_round(0, 0, c)
            for c in range(WO_AHEAD):
                wo_round(0, 0, c)
            x1t_round(0, 2, 0)
            x1t_round(0, 3, 0)
            for c in range(EARLY):
                gelu(0, c, 0)

            def tile(t, parity, bt, bu):
                more = bu is not None
                for c in range(CH):
                    if more and c in SPLIT_AT:
                        x1t_round(t + 1, SPLIT_AT.index(c), 1 - parity)
                    if more and c in (0, 1):
                        xt_round(t + 1, 2 * c)
                        xt_round(t + 1, 2 * c + 1)
                    if more or c + WI_AHEAD < CH:
                        wi_round(*ahead(t, bt, bu, c + WI_AHEAD))
                    if more or c + WO_AHEAD < CH:
                        wo_round(*ahead(t, bt, bu, c + WO_AHEAD))
                    if isinstance(t, int) and t == 0 and c + 2 < EARLY:
                        pass
                    elif c + 2 < CH:
                        gelu(t, c + 2, parity)
                    elif more:
                        gelu(t + 1, c + 2 - CH, 1 - parity)
                    if more and c == 1:
                        hidden(t + 1)
                    if isinstance(t, int) and t == 0 and c == 3:
                        fold_round(1)

            for_tiles(act, tile)
            def center(s):
                act.wait_ge(negmean_ready, s + 1)
                r = rows[:, 1, s, :]
                act.activation(r, r, ACT.Identity, bias=negmean[:, s:s + 1]).then_inc(act_centered, 1)

            def scale(s, count):
                act.wait_ge(times_gamma_done, count)
                act.wait_ge(rstd_ready[1], SUB * (TILES - 1) + s + 1)
                r = rows[:, 1, s, :]
                act.activation(r, r, ACT.Identity, scale=rstd[1][:, s:s + 1]).then_inc(act_scaled, 1)

            center(0)
            center(1)
            scale(0, 1)
            center(2)
            scale(2, 2)

        @block.vector
        def _(dve):
            steps = [0]

            def step(ins):
                steps[0] += 1
                ins.then_inc(setup_step, 1)
                dve.wait_ge(setup_step, steps[0])

            dve.wait_ge(ids_landed, 16)
            dve.tensor_scalar(idx[:, 0, :], ids[:, 0, :], 0.0, float(E0 - 1), ALU.max, ALU.min).then_inc(idx_ready, 1)
            step(dve.tensor_scalar(ids[:, 2, :], ids[:, 1, :], 0.0, float(E1), ALU.is_lt, ALU.mult))
            step(dve.tensor_tensor(ids[:, 3, :], ids[:, 1, :], ids[:, 2, :], ALU.add))
            dve.tensor_scalar(idx[:, 1, :], ids[:, 3, :], 0.0, float(E1 - 1), ALU.max, ALU.min).then_inc(idx_ready, 1)

            def split(dst_hi, dst_lo, src):
                step(dve.tensor_copy(dst_hi, src))
                step(dve.tensor_tensor(dst_lo, src, dst_hi.bitcast(F32), ALU.subtract))

            def chunks(a, n=KD):
                return a.rearrange("p (k i) -> p k i", k=n)

            def xt_rest(u, k):
                dve.wait_ge(xt_hi, KD * u + k + 1)
                part = xt_part(u, k)
                dve.tensor_tensor(part[:, 1], xt_raw[:, k, :], part[:, 0].bitcast(F32),
                                  ALU.subtract).then_inc(xt_split, 1)

            def hid_rest(u):
                dve.wait_ge(hid_hi, u + 1)
                dve.tensor_tensor(hid[:, 1, :], ps0[:, 0, :], hid[:, 0, :].bitcast(F32),
                                  ALU.subtract).then_inc(hid_split, 1)

            def fold_rest(b):
                dve.wait_ge(fold_hi, b + 1)
                dve.tensor_tensor(fold_w[:, b, 1, :], ps0[:, 1, :], fold_w[:, b, 0, :].bitcast(F32),
                                  ALU.subtract).then_inc(fold_split, 1)

            def up_bias(b, bank):
                dve.wait_ge(bias_done, b + 1)
                dve.tensor_tensor(up_b[:, b, :], bank, up_b[:, 1, :], ALU.add).then_inc(up_b_ready, 1)

            def normalize(blk, t, subs, row, gamma, beta, eps, done):
                for s in subs:
                    dve.wait_ge(sum_ready[blk], SUB * t + s + 1)
                    dve.bn_stats(stats[blk][:, s, :], row(s)).then_inc(stats_ready[blk], 1)
                for s in subs:
                    dve.wait_ge(stats_ready[blk], SUB * t + s + 1)
                    dve.sem_inc(stats_seen[blk], 1)
                    dve.bn_aggr(mv[blk][:, s, :], stats[blk][:, s, :]).then_inc(mv_ready[blk], 1)
                for s in subs:
                    dve.wait_ge(mv_ready[blk], SUB * t + s + 1)
                    dve.tensor_scalar(var[blk][:, s:s + 1], mv[blk][:, s, 1:2], eps, None,
                                      ALU.add).then_inc(var_ready[blk], 1)
                for s in subs:
                    dve.scalar_tensor_tensor(out=row(s), in0=row(s), scalar=mv[blk][:, s, 0:1], in1=gamma,
                                             op0=ALU.subtract, op1=ALU.mult).then_inc(centered[blk], 1)
                for s in subs:
                    before = SUB - 1 if isinstance(t, int) and blk == 1 and t == TILES - 1 else 0
                    dve.wait_ge(centered[blk], SUB * t + s + 1 - before)
                    dve.wait_ge(rstd_ready[blk], SUB * t + s + 1)
                    dve.scalar_tensor_tensor(out=row(s), in0=row(s), scalar=rstd[blk][:, s:s + 1], in1=beta,
                                             op0=ALU.mult, op1=ALU.add).then_inc(done, 1)

            def adapter_sum(u, s, parity, bank):
                r = rows[:, parity, s, :]
                dve.wait_ge(up_done, SUB * u + s + 1)
                dve.wait_ge(xb_ready, SUB * u + s + 1)
                dve.tensor_tensor(r, bank, r, ALU.add).then_inc(sum_ready[0], 1)

            def adapter_rows(u, subs, parity):
                normalize(0, u, subs, lambda s: rows[:, parity, s, :], g0, be0, EPS0, x1_ready)

            def turn_blocks(u, s, parity):
                dve.wait_ge(x1_ready, SUB * u + s + 1)
                for q in range(P // BLK):
                    for g in range(P // BLK):
                        src = chunks(rows[q * BLK:(q + 1) * BLK, parity, s, :])[:, :, g * BLK:(g + 1) * BLK]
                        dst = chunks(ps0[g * BLK:(g + 1) * BLK, s % 2, :])[:, :, q * BLK:(q + 1) * BLK]
                        last = dve.transpose(dst, src)
                last.then_inc(turned, 1)

            def x1t_rest(u, s, parity):
                dve.wait_ge(x1t_hi, SUB * u + s + 1)
                part = x1t[parity][:, :, :, s * P:(s + 1) * P]
                dve.tensor_tensor(part[:, 1], chunks(ps0[:, s % 2, :]), part[:, 0].bitcast(F32),
                                  ALU.subtract).then_inc(x1t_split, 1)

            def h_rest(t, c):
                dve.wait_ge(gelu_done, CH * t + c + 1)
                dve.tensor_tensor(h[:, c % H_RING, 1, :], hidden_bank(t, c), h[:, c % H_RING, 0, :].bitcast(F32),
                                  ALU.subtract).then_inc(h_split, 1)

            def take_acc(t, s, parity):
                if isinstance(t, int) and t == TILES - 1:
                    dve.wait_ge(mm2_done, SUB * (CH * t + CH - LATE) + (s + 1) * LATE + (s == 0))
                else:
                    dve.wait_ge(mm2_done, SUB * (CH * t + CH - 1) + s + 1)
                dve.wait_ge(res_ready, SUB * t + s + 1)
                r = rows[:, parity, s, :]
                dve.tensor_tensor(r, acc[:, s, :], r, ALU.add).then_inc(sum_ready[1], 1)

            def out_rows(t, bt, subs, parity):
                normalize(1, t, subs, lambda s: rows[:, parity, s, :], vec1[:, bt, 1, :], vec1[:, bt, 2, :],
                          EPS1, y_ready)

            def start_shared(t, s, parity):
                dve.wait_ge(sum_ready[1], SUB * t + s + 1)
                dve.bn_stats(stats[1][:, s, :], rows[:, parity, s, :]).then_inc(stats_ready[1], 1)
                dve.wait_ge(stats_ready[1], SUB * t + s + 1)
                dve.bn_aggr(mv[1][:, s, :], stats[1][:, s, :]).then_inc(mv_ready[1], 1)
                dve.wait_ge(mv_ready[1], SUB * t + s + 1)
                dve.tensor_scalar(negmean[:, s:s + 1], mv[1][:, s, 0:1], -1.0, None, ALU.mult).then_inc(negmean_ready, 1)
                dve.tensor_scalar(var[1][:, s:s + 1], mv[1][:, s, 1:2], EPS1, None, ALU.add).then_inc(var_ready[1], 1)

            def end_shared(t, s, parity):
                dve.wait_ge(act_centered, s + 1)
                dve.wait_ge(rstd_ready[1], SUB * t + s + 1)
                r = rows[:, parity, s, :]
                dve.scalar_tensor_tensor(out=r, in0=r, scalar=rstd[1][:, s:s + 1], in1=vec1[:, BATCH - 1, 1, :],
                                         op0=ALU.mult, op1=ALU.mult).then_inc(dve_scaled, 1)

            def expert_matrix(b):
                dve.wait_ge(down_w_ready, 1)
                step(dve.tensor_scalar(exp_off[:, :], ident[:, :], valid[:, 1, b:b + 1], None, ALU.mult))
                dve.wait_ge(exp_landed[b], 16)
                w = exp_raw[:, b, 0:A]
                step(dve.scalar_tensor_tensor(out=w, in0=w, scalar=valid[:, 0, b:b + 1], in1=exp_off[:, :],
                                              op0=ALU.mult, op1=ALU.add))
                step(dve.tensor_copy(exp_w[:, 0, :], w))
                dve.tensor_tensor(exp_w[:, 1, :], w, exp_w[:, 0, :].bitcast(F32), ALU.subtract).then_inc(exp_w_ready, 1)
                step(dve.tensor_tensor(hid_b[:, :], exp_raw[:, b, A:A + 1], valid[:, 0, b:b + 1], ALU.mult))
                step(dve.tensor_tensor(hid_b[:, :], hid_b[:, :], exp_raw[:, b, A + 1:A + 2], ALU.add))
                wide = hid_b[:, :].to_broadcast([P, P])
                step(dve.tensor_copy(exp_b[:, 0, :], wide))
                dve.tensor_tensor(exp_b[:, 1, :], wide, exp_b[:, 0, :].bitcast(F32), ALU.subtract).then_inc(exp_b_ready, 1)

            dve.wait_ge(down_landed, 16)
            dve.tensor_copy(down_w[:, 0, :, :], chunks(down_raw[:, 0:D])).then_inc(down_w_hi, 1)
            for k in range(KD):
                xt_rest(0, k)
                if k == 1:
                    dve.wait_ge(ids_all_landed, 16)
                    step(dve.tensor_scalar(valid[:, 0, :], ids_all[:, :], 0.0, None, ALU.is_ge))
                    step(dve.tensor_scalar(valid[:, 1, :], ids_all[:, :], float(E0), None, ALU.is_lt))
                    step(dve.tensor_tensor(valid[:, 0, :], valid[:, 0, :], valid[:, 1, :], ALU.mult))
                    step(dve.tensor_scalar(valid[:, 1, :], valid[:, 0, :], -1.0, 1.0, ALU.mult, ALU.add))
            dve.wait_ge(const_ready, 3)
            expert_matrix(0)
            hid_rest(0)
            fold_rest(0)
            adapter_sum(0, 0, 0, acc[:, 0, :])
            adapter_sum(0, 1, 0, acc[:, 1, :])
            dve.wait_ge(vec0_landed, 16)
            adapter_rows(0, (0, 1), 0)
            adapter_sum(0, 2, 0, acc[:, 2, :])
            dve.wait_ge(up_b_landed, 16)
            up_bias(0, ps_h[:, 0, :])
            x1t_rest(0, 0, 0)
            x1t_rest(0, 1, 0)
            adapter_sum(0, 3, 0, acc[:, 3, :])
            adapter_rows(0, (2, 3), 0)
            x1t_rest(0, 2, 0)
            x1t_rest(0, 3, 0)
            dve.wait_ge(ffn_landed[0], 32)
            dve.tensor_copy(bi_now[:, 0, :], bi[:, 0, :]).then_inc(bi_now_ready, 1)
            for c in range(EARLY):
                h_rest(0, c)

            def tile(t, parity, bt, bu):
                more = bu is not None
                for c in range(CH):
                    if more and c in (0, 1):
                        xt_rest(t + 1, 2 * c)
                        xt_rest(t + 1, 2 * c + 1)
                    if more and c == 0:
                        dve.tensor_copy(bi_now[:, 1 - parity, :], bi[:, bu, :]).then_inc(bi_now_ready, 1)
                    if more and c == 2:
                        hid_rest(t + 1)
                    if c == 2 and isinstance(t, int) and t == 0:
                        expert_matrix(1)
                    if c == 4 and isinstance(t, int) and t == 0:
                        fold_rest(1)
                    if c == 5 and isinstance(t, int) and t == 0:
                        up_bias(1, ps0[:, 1, :])
                    if c in (1, 2, 3, 4) and not (isinstance(t, int) and t == 0):
                        out_rows(t - 1, (t - 1) // PER_BATCH, (c - 1,), 1 - parity)
                    if c == 9 and isinstance(t, int) and t == 0:
                        dve.wait_ge(ffn_landed[1], 32)
                    if more and c in SPLIT_AT:
                        x1t_rest(t + 1, SPLIT_AT.index(c), 1 - parity)
                    if more and c in NORM_AT:
                        s = NORM_AT.index(c)
                        adapter_sum(t + 1, s, 1 - parity, ps0[:, s % 2, :])
                        adapter_rows(t + 1, (s,), 1 - parity)
                    if more and c in TURN_AT:
                        turn_blocks(t + 1, TURN_AT.index(c), 1 - parity)
                    if isinstance(t, int) and t == 0 and c + 2 < EARLY:
                        pass
                    elif more or c + 2 < CH:
                        h_rest(*ahead(t, bt, bu, c + 2)[::2])
                for s in range(SUB):
                    take_acc(t, s, parity)
                    if not more and s < SUB - 1:
                        if s == 2:
                            end_shared(t, 1, parity)
                        start_shared(t, s, parity)
                    elif not more:
                        out_rows(t, BATCH - 1, (s,), parity)

            for_tiles(dve, tile)

        @block.tensor
        def _(pe):
            def three(out, left, right, start, stop):
                pe.matmul(out, left[0], right[0], start=start, stop=False)
                pe.matmul(out, left[0], right[1], start=False, stop=False)
                return pe.matmul(out, left[1], right[0], start=False, stop=stop)

            def up_products(bank, c, parity, a, b):
                for k in range(KD):
                    last = three(bank[:, a:b], [wi[:, c % WI_RING, i, k, :] for i in (0, 1)],
                                 [x1t[parity][:, i, k, a:b] for i in (0, 1)], k == 0, k == KD - 1)
                return last

            def up_layer(t, c, parity):
                n = CH * t + c
                pe.wait_ge(wi_lo, n + 1)
                if c == 0:
                    pe.wait_ge(x1t_split, SUB * (t + 1))
                wait(pe, h_split, n - 1)
                up_products(ps_h[:, c % 2, :], c, parity, 0, TOK).then_inc(mm1_done, 1)

            def down_product(c, s):
                three(acc[:, s, :], [h[:, c % H_RING, i, s * P:(s + 1) * P] for i in (0, 1)],
                      [wo[:, c % WO_RING, i, :] for i in (0, 1)], c == 0, c == CH - 1).then_inc(mm2_done, 1)

            def down_layer(t, c):
                n = CH * t + c
                pe.wait_ge(wo_lo, n + 1)
                pe.wait_ge(h_split, n + 1)
                first = isinstance(t, int) and t == 0 and c == 0
                for s in (2, 3, 0, 1) if first else range(SUB):
                    if first and s < 2:
                        pe.wait_ge(h_split, s + 3)
                    elif c == 0:
                        wait(pe, sum_ready[1], SUB * (t - 1) + s + 1)
                    down_product(c, s)

            def adapter_down(u, k):
                pe.wait_ge(xt_split, KD * u + k + 1)
                if k == 0:
                    wait(pe, x1t_split, SUB * u - 1)
                three(ps0[:, 0, :], [down_w[:, i, k, :] for i in (0, 1)], [xt_part(u, k)[:, i] for i in (0, 1)],
                      k == 0, k == KD - 1).then_inc(down_done, 1)

            def fold_product(b):
                pe.wait_ge(exp_w_ready, b + 1)
                pe.wait_ge(up_w_ready, 1)
                wait(pe, x1t_split, SUB * b)
                three(ps0[:, 1, :], [exp_w[:, i, :] for i in (0, 1)], [up_w[:, i, :] for i in (0, 1)],
                      True, True).then_inc(fold_done, 1)

            def bias_product(b, bank, alone=True):
                pe.wait_ge(exp_b_ready, b + 1)
                return three(bank, [exp_b[:, i, :] for i in (0, 1)], [up_w[:, i, :] for i in (0, 1)], True, alone)

            def adapter_up(u, bu, s, bank, alone=True):
                pe.wait_ge(hid_split, u + 1)
                three(bank, [hid[:, i, s * P:(s + 1) * P] for i in (0, 1)],
                      [fold_w[:, bu, i, :] for i in (0, 1)], alone, True).then_inc(up_done, 1)

            def turn(s):
                pe.wait_ge(x1_ready, s + 1)
                for k in range(KD):
                    last = pe.transpose(ps0[:, s % 2, k * P:(k + 1) * P], rows[:, 0, s, k * P:(k + 1) * P], ident[:, :])
                last.then_inc(turned, 1)

            def keep_warm(n, bank):
                for _ in range(n):
                    pe.matmul(bank[:, 0:P], ident[:, :], ident[:, :], start=True, stop=True)

            def early_products(c, s):
                pe.wait_ge(wi_lo, c + 1)
                return up_products(hidden_bank(0, c), c, 0, (s - 1) * P, (s + 1) * P)

            pe.wait_ge(const_ready, 3)
            keep_warm(WARM[0], ps_h[:, 1, :])
            pe.wait_ge(down_w_ready, 1)
            for k in range(KD):
                adapter_down(0, k)
            keep_warm(WARM[1], ps_h[:, 1, :])
            fold_product(0)
            for s in range(SUB):
                if s % 2 == 0:
                    for i in (s, s + 1):
                        bias_product(0, acc[:, i, :], alone=False)
                pe.wait_ge(fold_split, 1)
                adapter_up(0, 0, s, acc[:, s, :], alone=False)
            bias_product(0, ps_h[:, 0, :]).then_inc(bias_done, 1)
            keep_warm(WARM[2], ps_h[:, 1, :])
            turn(0)
            turn(1)
            keep_warm(WARM[3], ps_h[:, 1, :])
            pe.wait_ge(x1t_split, 2)
            pe.wait_ge(up_b_ready, 1)
            for c in range(EARLY - 1):
                early_products(c, 1)
            turn(2)
            turn(3)
            early_products(EARLY - 1, 1)
            pe.wait_ge(x1t_split, SUB)
            for c in range(EARLY):
                early_products(c, SUB - 1).then_inc(mm1_done, 1)

            def tile(t, parity, bt, bu):
                more = bu is not None
                for c in range(CH):
                    early = isinstance(t, int) and t == 0 and c + 2 < EARLY
                    if early:
                        pass
                    elif c + 2 < CH:
                        up_layer(t, c + 2, parity)
                    elif more:
                        up_layer(t + 1, c + 2 - CH, 1 - parity)
                    if early:
                        down_layer(t, c)
                    if more and c in (0, 1):
                        adapter_down(t + 1, 2 * c)
                        adapter_down(t + 1, 2 * c + 1)
                    if c == 3 and isinstance(t, int) and t == 0:
                        fold_product(1)
                    if c == 4 and isinstance(t, int) and t == 0:
                        pe.wait_ge(fold_split, 2)
                        bias_product(1, ps0[:, 1, :]).then_inc(bias_done, 1)
                    if more and c in UP_AT:
                        s = UP_AT.index(c)
                        if s:
                            pe.wait_ge(x1t_split, SUB * (t + 1) + s - 1)
                        if s == 1 and isinstance(t, int) and t == 0:
                            pe.wait_ge(up_b_ready, 2)
                        adapter_up(t + 1, bu, s, ps0[:, s % 2, :])
                    if early:
                        pass
                    elif more or c < CH - LATE:
                        down_layer(t, c)
                    elif c == CH - 1:
                        order = [(s, j) for s in range(SUB) for j in range(CH - LATE, CH)]
                        order[LATE - 1:LATE + 1] = order[LATE:LATE - 2:-1]
                        for s, j in order:
                            if s == 0:
                                pe.wait_ge(wo_lo, CH * t + j + 1)
                                pe.wait_ge(h_split, CH * t + j + 1)
                            down_product(j, s)

            for_tiles(pe, tile)


def kernel(x, itok_B_0_15, itok_B_0_7, L0_cond_down_W, L0_cond_down_b, L0_cond_up_W, L0_cond_up_b,
           L0_cond_expert_W, L0_cond_expert_b, L0_cond_domain_emb, L0_cond_ln_gamma, L0_cond_ln_beta,
           L1_cond_Wi, L1_cond_bi, L1_cond_Wo, L1_cond_bo, L1_cond_gamma, L1_cond_beta):
    import numpy as np
    import concourse.bacc as bacc
    from concourse.bass_utils import run_bass_kernel_spmd

    x = np.asarray(x)
    wi = np.asarray(L1_cond_Wi).reshape(E1, KD, P, CH, P).transpose(0, 3, 2, 1, 4).reshape(E1, CH, P, 1, D)
    wo = np.asarray(L1_cond_Wo).reshape(E1, CH, P, 1, D)
    arrays = {
        "xT": x.reshape(TILES, TOK, KD, P).transpose(0, 3, 2, 1),
        "x": x.reshape(TILES, SUB, P, D),
        "ids": np.concatenate([np.asarray(itok_B_0_15), np.asarray(itok_B_0_7)]).reshape(1, 2 * BATCH),
        "down": np.concatenate([np.asarray(L0_cond_down_W).reshape(A, KD, P).transpose(2, 1, 0).reshape(P, KD * A),
                                np.asarray(L0_cond_down_b).reshape(A, 1)], axis=1),
        "up_w": np.asarray(L0_cond_up_W).T,
        "exp": np.concatenate([np.asarray(L0_cond_expert_W),
                               np.asarray(L0_cond_expert_b).reshape(E0, A, 1),
                               np.asarray(L0_cond_domain_emb).reshape(E0, A, 1)], axis=2),
        "vec0": np.stack([np.asarray(L0_cond_up_b), np.asarray(L0_cond_ln_gamma),
                          np.asarray(L0_cond_ln_beta)]).reshape(1, 3, D),
        "w": np.concatenate([wi, wo], axis=3),
        "bi": np.asarray(L1_cond_bi).reshape(E1, CH, P).transpose(0, 2, 1),
        "vec1": np.stack([np.asarray(L1_cond_bo), np.asarray(L1_cond_gamma),
                          np.asarray(L1_cond_beta)], axis=1).reshape(E1, 1, 3, D),
    }
    nc = bacc.Bacc("TRN2", target_bir_lowering=False, num_devices=1, dynamic_dma_scratch_size=1024)
    ins, args = {}, []
    for name, a in arrays.items():
        a = np.ascontiguousarray(a)
        ins[f"in_{name}"] = a
        args.append(nc.dram_tensor(f"in_{name}", a.shape, mybir.dt.from_np(a.dtype), kind="ExternalInput").ap())
    args.append(nc.dram_tensor("out", (TILES, SUB, P, D), F32, kind="ExternalOutput").ap())
    adapter_ffn(nc, *args)
    got = run_bass_kernel_spmd(nc, [ins], core_ids=[0]).results[0]["out"]
    return got.reshape(BATCH, SEQ, D)
```
